# Optimizing a Trainium2 kernel written in Bass

```python
import numpy as np
import jax
import jax.numpy as jnp

def _softmax(x, axis=-1):
    return jax.nn.softmax(x, axis=axis)

def _gelu(x):
    return jax.nn.gelu(x, approximate=True)

def _silu(x):
    return jax.nn.silu(x)

def _sigmoid(x):
    return jax.nn.sigmoid(x)

def _layernorm(x, axis=-1, eps=1e-05):
    m = jnp.mean(x, axis=axis, keepdims=True)
    v = jnp.var(x, axis=axis, keepdims=True)
    return (x - m) / jnp.sqrt(v + eps)

def _scatter_add(tgt, idx, src, axis=0):
    return tgt.at[idx].add(src)

def _segment_sum(src, seg, n):
    return jax.ops.segment_sum(src, seg, n)
kernel_name = 'mk_seq_postln_d1_jaxref_r4_5eac0b'

def setup_inputs(seed: int=0):
    np.random.seed(seed)
    _w = jnp.asarray

    def _L0_attn_setup():
        import jax, jax.numpy as jnp
        import numpy as np
        D_MODEL = 256
        NUM_HEADS = 16
        D_K = 256
        D_V = 256
        D_IN = 256
        THETA = 10000.0
        B, S = (2, 512)

        def _rope(t, theta):
            hd = t.shape[-1]
            inv_freq = 1.0 / theta ** (jnp.arange(0, hd, 2, dtype=jnp.float32) / hd)
            pos = jnp.arange(t.shape[-2], dtype=jnp.float32)
            ang = pos[:, None] * inv_freq[None, :]
            cos, sin = (jnp.cos(ang), jnp.sin(ang))
            tp = t.reshape(t.shape[:-1] + (hd // 2, 2))
            t0, t1 = (tp[..., 0], tp[..., 1])
            out = jnp.stack([t0 * cos - t1 * sin, t0 * sin + t1 * cos], axis=-1)
            return out.reshape(t.shape)
        key = jax.random.key(seed)
        k1, k2, k3, k4, k5 = jax.random.split(key, 5)
        std_qkv = (2.0 / (D_IN + D_K)) ** 0.5
        std_o = (2.0 / (D_V + D_MODEL)) ** 0.5
        x = jax.random.normal(k1, (B, S, D_IN), jnp.float32)
        wq = jax.random.normal(k2, (D_IN, D_K), jnp.float32) * std_qkv
        wk = jax.random.normal(k3, (D_IN, D_K), jnp.float32) * std_qkv
        wv = jax.random.normal(k4, (D_IN, D_V), jnp.float32) * std_qkv
        wo = jax.random.normal(k5, (D_V, D_MODEL), jnp.float32) * std_o
        return {'x': x, 'wq': wq, 'wk': wk, 'wv': wv, 'wo': wo}
    _L0_attn_in = _L0_attn_setup()

    def _L0_ffn_setup():
        import jax, jax.numpy as jnp
        import numpy as np
        import math
        D_IN = 256
        FEATURES = (1024, 1024, 256)
        BATCH, SEQ = (8, 512)

        def _conn_dense(kernel_bool, x):
            w = jnp.where(kernel_bool, jnp.float32(1.0), jnp.float32(-1.0))
            return x @ w
        key = jax.random.key(seed)
        kx, kk0, kk1, kk2 = jax.random.split(key, 4)
        x = jax.random.normal(kx, (BATCH, SEQ, D_IN), dtype=jnp.float32)
        k0 = jax.random.randint(kk0, (2 * D_IN, FEATURES[0]), 0, 2).astype(jnp.bool_)
        k1 = jax.random.randint(kk1, (FEATURES[0], FEATURES[1]), 0, 2).astype(jnp.bool_)
        k2 = jax.random.randint(kk2, (FEATURES[1], FEATURES[2]), 0, 2).astype(jnp.bool_)
        s0 = jnp.asarray(1.0 / math.sqrt(2 * D_IN), dtype=jnp.float32)
        s1 = jnp.asarray(1.0 / math.sqrt(FEATURES[0]), dtype=jnp.float32)
        s2 = jnp.asarray(1.0 / math.sqrt(FEATURES[1]), dtype=jnp.float32)
        return {'x': x, 'k0': k0, 'k1': k1, 'k2': k2, 's0': s0, 's1': s1, 's2': s2}
    _L0_ffn_in = _L0_ffn_setup()
    _d = {'L0_attn_x': _L0_attn_in['x'], 'L0_attn_wq': _L0_attn_in['wq'], 'L0_attn_wk': _L0_attn_in['wk'], 'L0_attn_wv': _L0_attn_in['wv'], 'L0_attn_wo': _L0_attn_in['wo'], 'L0_ffn_k0': _L0_ffn_in['k0'], 'L0_ffn_k1': _L0_ffn_in['k1'], 'L0_ffn_k2': _L0_ffn_in['k2'], 'L0_ffn_s0': _L0_ffn_in['s0'], 'L0_ffn_s1': _L0_ffn_in['s1'], 'L0_ffn_s2': _L0_ffn_in['s2']}
    _x0 = _d['L0_attn_x']
    _d['L0_attn_x'] = jax.random.normal(jax.random.fold_in(jax.random.key(seed), 1), (8, 1024, 256), dtype=_x0.dtype)
    del _x0
    return _d

def reference(L0_attn_x, L0_attn_wq, L0_attn_wk, L0_attn_wv, L0_attn_wo, L0_ffn_k0, L0_ffn_k1, L0_ffn_k2, L0_ffn_s0, L0_ffn_s1, L0_ffn_s2):

    def _L0_attn_ref(x, wq, wk, wv, wo):
        import jax, jax.numpy as jnp
        import numpy as np
        D_MODEL = 256
        NUM_HEADS = 16
        D_K = 256
        D_V = 256
        D_IN = 256
        THETA = 10000.0
        B, S = (2, 512)

        def _rope(t, theta):
            hd = t.shape[-1]
            inv_freq = 1.0 / theta ** (jnp.arange(0, hd, 2, dtype=jnp.float32) / hd)
            pos = jnp.arange(t.shape[-2], dtype=jnp.float32)
            ang = pos[:, None] * inv_freq[None, :]
            cos, sin = (jnp.cos(ang), jnp.sin(ang))
            tp = t.reshape(t.shape[:-1] + (hd // 2, 2))
            t0, t1 = (tp[..., 0], tp[..., 1])
            out = jnp.stack([t0 * cos - t1 * sin, t0 * sin + t1 * cos], axis=-1)
            return out.reshape(t.shape)
        b, s, _ = x.shape
        hd = D_K // NUM_HEADS
        hdv = D_V // NUM_HEADS
        q = jnp.einsum('bsd,de->bse', x, wq).reshape(b, s, NUM_HEADS, hd).transpose(2, 0, 1, 3)
        k = jnp.einsum('bsd,de->bse', x, wk).reshape(b, s, NUM_HEADS, hd).transpose(2, 0, 1, 3)
        v = jnp.einsum('bsd,de->bse', x, wv).reshape(b, s, NUM_HEADS, hdv).transpose(2, 0, 1, 3)
        q = _rope(q, THETA)
        k = _rope(k, THETA)
        scale = 1.0 / jnp.sqrt(jnp.asarray(hd, jnp.float32))
        scores = jnp.einsum('hbqd,hbkd->hbqk', q, k) * scale
        causal = jnp.tril(jnp.ones((s, s), dtype=bool))
        scores = jnp.where(causal, scores, -jnp.inf)
        attn = jax.nn.softmax(scores, axis=-1)
        o = jnp.einsum('hbqk,hbkd->hbqd', attn, v)
        o = o.transpose(1, 2, 0, 3).reshape(b, s, D_V)
        return jnp.einsum('bsd,de->bse', o, wo)

    def _L0_ffn_ref(x, k0, k1, k2, s0, s1, s2):
        import jax, jax.numpy as jnp
        import numpy as np
        import math
        D_IN = 256
        FEATURES = (1024, 1024, 256)
        BATCH, SEQ = (8, 512)

        def _conn_dense(kernel_bool, x):
            w = jnp.where(kernel_bool, jnp.float32(1.0), jnp.float32(-1.0))
            return x @ w
        h = jnp.concatenate([x, -x], axis=-1)
        h = s0 * _conn_dense(k0, h)
        h = jax.nn.relu(h) * 2
        h = s1 * _conn_dense(k1, h)
        h = jax.nn.relu(h) * 2
        h = s2 * _conn_dense(k2, h)
        return h
    x = L0_attn_x
    x = _layernorm(x + _L0_attn_ref(x, L0_attn_wq, L0_attn_wk, L0_attn_wv, L0_attn_wo), axis=-1)
    x = _layernorm(x + _L0_ffn_ref(x, L0_ffn_k0, L0_ffn_k1, L0_ffn_k2, L0_ffn_s0, L0_ffn_s1, L0_ffn_s2), axis=-1)
    return x

_drawn_inputs = setup_inputs


def setup_inputs(seed=0):
    import zlib

    import numpy as np

    out = dict(_drawn_inputs(seed))
    spreads = {}
    factors = {}
    for name, (base, spread) in spreads.items():
        noise = np.random.default_rng([zlib.crc32(name.encode()), seed]).standard_normal(out[name].shape)
        drawn = base * np.exp(spread * noise) if base else spread * noise
        out[name] = jnp.asarray(drawn.astype(out[name].dtype))
    for name, factor in factors.items():
        out[name] = (out[name] * factor).astype(out[name].dtype)
    return out
```

```python
from contextlib import ExitStack

import concourse.bass as bass
from concourse import mybir
import numpy as np

F32, BF16, F16, U8 = mybir.dt.float32, mybir.dt.bfloat16, mybir.dt.float16, mybir.dt.uint8
ALU, ACT, AX = mybir.AluOpType, mybir.ActivationFunctionType, mybir.AxisListType

P = 128
B, S, D = 8, 1024, 256
H, HD = 16, 16
T = S // P
F = 1024
HG = 4
G = H // HG
NC = D // P
BANK = 512
EPS = 1e-5
LOWEST = -3.0e38
SCALE = float(HD) ** -0.5
Q_PARTS = (0, 1, 2, 0, 1, 0)
K_PARTS = (0, 0, 0, 1, 1, 2)
KR = HD * len(Q_PARTS)
KM = KR + 3
W1_SCALE = 1.0 / 16
OUT_FACTOR = 2.0 * 2.0 * 2.0 / W1_SCALE

ST_UNITS = (
    ((0, 0, 512, 0),),
    ((0, 512, 1024, 0),),
    ((1, 128, 512, 0), (7, 896, 1024, 384)),
    ((2, 256, 512, 0), (6, 768, 1024, 256)),
    ((3, 384, 512, 0), (5, 640, 1024, 128)),
    ((4, 512, 1024, 0),),
    ((1, 512, 1024, 0),),
    ((2, 512, 1024, 0),),
    ((3, 512, 1024, 0),),
)
NU = len(ST_UNITS)
DIAG = tuple(tuple(c for k, a, b, c in u if a == k * P) for u in ST_UNITS)
MASKED = tuple(u for u in range(NU) if DIAG[u])
MX_UNITS = (
    ((7, 0, 512, 0),),
    ((7, 512, 1024, 0),),
    ((6, 0, 512, 0),),
    ((6, 512, 896, 0), (0, 0, 128, 384)),
    ((5, 0, 512, 0),),
    ((5, 512, 768, 0), (1, 0, 256, 256)),
    ((4, 0, 512, 0),),
    ((3, 0, 512, 0),),
    ((2, 0, 384, 0), (4, 512, 640, 384)),
)
NMX = len(MX_UNITS)
MX_AT = (0, 5, 5, 6, 6, 6, 6, 2, 0)
LAG = 2
RING = 3


def st_ring():
    uses = []
    for g in range(G):
        for u in range(NU):
            uses += [("st", g, u, 0), ("st", g, u, 1)]
            if u == 3 and g > 0:
                uses.append(("ot", g - 1, 0, 0))
    uses.append(("ot", G - 1, 0, 0))
    return uses


ST_RING = st_ring()
SLOT = {use: i for i, use in enumerate(ST_RING)}


def build(nc, x, wq, wk, wv, wo, k0, k1, k2, s0, s1, s2, cos, sin, ident, tri, out, scratch):
    with ExitStack() as ctx:
        def sb(name, shape, dt):
            return ctx.enter_context(nc.sbuf_tensor(name, shape, dt))

        def sem(name):
            return ctx.enter_context(nc.semaphore(name))

        psum = ctx.enter_context(nc.psum_tensor("psum", [P, 8, BANK], F32))

        w_qkv = sb("w_qkv", [P, NC, 3, D], F32)
        w_o = sb("w_o", [P, NC, D], F32)
        w0 = sb("w0", [P, NC, F], F16)
        w1 = sb("w1", [P, F // P, F], F16)
        w2 = sb("w2", [P, F // P, D], F16)
        cos_sb = sb("cos_sb", [P, S], F32)
        sin_sb = sb("sin_sb", [P, S], F32)
        id_sb = sb("id_sb", [P, P], F32)
        tri_sb = sb("tri_sb", [P, P], F32)
        s_in = sb("s_in", [P, 3], F32)
        s_sign = sb("s_sign", [P, 3], F32)
        s_abs = sb("s_abs", [P, 3], F32)
        s_prod = sb("s_prod", [P, 1], F32)
        factor = sb("factor", [P, 1], F32)
        minus_half = sb("minus_half", [P, T], F32)
        x_in = sb("x_in", [P, T, D], F32)
        x_res = sb("x_res", [P, T, D], F32)
        x1 = sb("x1", [P, T, D], F32)
        v_ones = sb("v_ones", [P, T, H, 32], F32)
        parts = sb("parts", [P, 2, 3, S], BF16)
        q_st = sb("q_st", [P, 2, HG, S], BF16)
        k_st = sb("k_st", [P, 2, HG, S], BF16)
        rope_buf = sb("rope_buf", [P, 3, S], F32)
        swapped, turned, rest = rope_buf[:, 0, :], rope_buf[:, 1, :], rope_buf[:, 2, :]
        region = sb("region", [P, 8192], F32)
        probs = region[:, 0:RING * HG * BANK].rearrange("p (r j n) -> p r j n", r=RING, j=HG)
        x_t = region[:, 6144:8192].rearrange("p (c n) -> p c n", c=NC)
        halves = region[:, :].bitcast(F16).rearrange("p (a f n) -> p a f n", a=4, f=F // P)
        h1, h2 = (halves[:, 0], halves[:, 1]), (halves[:, 2], halves[:, 3])
        bits = region[:, :].bitcast(U8)
        k0_u8 = bits[:, 0:4 * F].rearrange("p (c n) -> p c n", c=4)
        k1_u8 = bits[:, 4 * F:12 * F].rearrange("p (c n) -> p c n", c=8)
        k2_u8 = bits[:, 12 * F:14 * F].rearrange("p (c n) -> p c n", c=8)
        o_t = sb("o_t", [P, S], F32)
        attn = sb("attn", [P, T, D], F32)
        attn_t = rope_buf[:, 0:2, :]
        x1_hi = sb("x1_hi", [P, NC, S], F16)
        x1_lo = sb("x1_lo", [P, NC, S], F16)
        y = sb("y", [P, 4, D], F32)
        recip = sb("recip", [P, T, HG], F32)
        mx = sb("mx", [P, 2, HG, T, 3], F32)
        m_col = sb("m_col", [P, P], F32)
        m_rest = sb("m_rest", [HG * T, P], F32)
        m_parts = sb("m_parts", [HG * T, 3, P], BF16)
        dump = sb("dump", [P, 4, P], BF16)
        stats = sb("stats", [P, T, 6], F32)
        mean_var = sb("mean_var", [P, T, 2], F32)
        var_eps = sb("var_eps", [P, T], F32)
        rstd = sb("rstd", [P, T], F32)
        stats2 = sb("stats2", [P, 4, 6], F32)
        mean_var2 = sb("mean_var2", [P, 4, 2], F32)
        var_eps2 = sb("var_eps2", [P, 4], F32)
        rstd2 = sb("rstd2", [P, 4], F32)

        consts_in = sem("consts_in")
        w_in = sem("w_in")
        x_loaded = sem("x_loaded")
        x_kept = sem("x_kept")
        xt_mm, xt_copied = sem("xt_mm"), sem("xt_copied")
        v_mm, v_copied = sem("v_mm"), sem("v_copied")
        qk_mm = sem("qk_mm")
        swap_done = sem("swap_done")
        cos_done = sem("cos_done")
        sin_done = sem("sin_done")
        turned_done = sem("turned_done")
        hi_done, rest_done, mid_done = sem("hi_done"), sem("rest_done"), sem("mid_done")
        parts_done = sem("parts_done")
        stored = [sem("stored0"), sem("stored1")]
        stacked = [sem("stacked0"), sem("stacked1")]
        mx_mm, mx_read = sem("mx_mm"), sem("mx_read")
        m_found = sem("m_found")
        m_mm = sem("m_mm")
        m_hi, m_taken, m_mid, m_split = sem("m_hi"), sem("m_taken"), sem("m_mid"), sem("m_split")
        m_rows = sem("m_rows")
        st_mm = sem("st_mm")
        exp_done = sem("exp_done")
        mask_done = sem("mask_done")
        pv_done = sem("pv_done")
        o_copied = sem("o_copied")
        ot_mm = sem("ot_mm")
        recip_done = sem("recip_done")
        normed = sem("normed")
        at_mm, at_copied = sem("at_mm"), sem("at_copied")
        wo_mm = sem("wo_mm")
        res_done, stat_done, aggr_done, eps_done, rstd_done, x1_done = (
            sem("res_done"), sem("stat_done"), sem("aggr_done"), sem("eps_done"), sem("rstd_done"), sem("x1_done"))
        x1t_mm, x1_hi_done, x1_lo_done = sem("x1t_mm"), sem("x1_hi_done"), sem("x1_lo_done")
        ff_mm = sem("ff_mm")
        h_hi, h_lo = sem("h_hi"), sem("h_lo")
        y_done, stat2_done, aggr2_done, eps2_done, rstd2_done, out_done = (
            sem("y_done"), sem("stat2_done"), sem("aggr2_done"), sem("eps2_done"), sem("rstd2_done"), sem("out_done"))
        out_stored = sem("out_stored")
        ready = sem("ready")
        pool_ready = sem("pool_ready")

        dve_passed, pool_passed, sp_passed = sem("dve_passed"), sem("pool_passed"), sem("sp_passed")

        NMASK = len(MASKED)
        MXG = HG * NMX

        block = ctx.enter_context(nc.Block())

        def batches(eng, prologue, body, epilogue):
            prologue()
            with eng.Fori(0, B - 1) as i:
                body(i)
            epilogue()

        @block.sync
        def _(sp):
            sp.sem_inc(out_stored, 16)
            sp.dma_start(id_sb[:, :], ident).then_inc(consts_in, 16)
            for c in range(NC):
                for n, w in enumerate((wv, wq, wk)):
                    sp.dma_start(w_qkv[:, c, n, :], w[c * P:(c + 1) * P, :]).then_inc(consts_in, 16)
            sp.dma_start(x_in[:, :, :], x[0].rearrange("(t p) d -> p t d", p=P)).then_inc(x_loaded, 16)
            sp.dma_start(cos_sb[:, :], cos).then_inc(consts_in, 16)
            sp.dma_start(sin_sb[:, :], sin).then_inc(consts_in, 16)
            sp.dma_start(tri_sb[:, :], tri).then_inc(consts_in, 16)
            sp.dma_start(w_o[:, :, :], wo.rearrange("(c p) n -> p c n", p=P)).then_inc(consts_in, 16)
            for n, s in enumerate((s0, s1, s2)):
                sp.dma_start(s_in[:, n:n + 1], s.partition_broadcast(P)).then_inc(w_in, 16)
            sp.dma_start(k0_u8, k0.rearrange("(c p) n -> p c n", p=P)).then_inc(w_in, 16)
            sp.dma_start(k1_u8, k1.rearrange("(c p) n -> p c n", p=P)).then_inc(w_in, 16)
            sp.dma_start(k2_u8, k2.rearrange("(c p) n -> p c n", p=P)).then_inc(w_in, 16)

            def store_parts(b, n):
                sp.wait_ge(parts_done, b * 4 + n + 1)
                sp.sem_inc(sp_passed, 1)
                sp.dma_start(scratch[n // 2, n % 2].rearrange("r p n -> p r n"), parts[:, n % 2, :, :])\
                    .then_inc(stored[n % 2], 16)

            def stack(b, g):
                c, row = g // 2, (g % 2) * HG * HD
                if row == 0:
                    for qk in range(2):
                        sp.wait_ge(stored[qk], b * 32 + 16 * c + 16)
                        sp.sem_inc(sp_passed, 1)
                if g >= 2:
                    sp.wait_ge(st_mm, b * 72 + 18 * (g - 1))
                    sp.sem_inc(sp_passed, 1)
                for r in range(len(Q_PARTS)):
                    for st, qk, part in ((q_st, 0, Q_PARTS[r]), (k_st, 1, K_PARTS[r])):
                        src = scratch[c, qk, part, row:row + HG * HD, :].rearrange("(j d) n -> d j n", d=HD)
                        sp.dma_start(st[r * HD:(r + 1) * HD, g % 2, :, :], src).then_inc(stacked[g % 2], 16)

            def max_rows(b, g):
                sp.wait_ge(m_split, b * 4 + g + 1)
                sp.sem_inc(sp_passed, 1)
                for r in range(3):
                    sp.dma_start(q_st[KR + r:KR + r + 1, g % 2, :, :].rearrange("p j (t n) -> p (j t) n", n=P),
                                 m_parts[:, r, :]).then_inc(m_rows, 16)

            def load_x(nxt):
                sp.wait_ge(x_kept, nxt)
                sp.sem_inc(sp_passed, 1)
                sp.wait_ge(xt_mm, nxt * 2)
                sp.sem_inc(sp_passed, 1)
                sp.dma_start(x_in[:, :, :], x[nxt].rearrange("(t p) d -> p t d", p=P)).then_inc(x_loaded, 16)

            def store_out(f, c):
                sp.wait_ge(out_done, f * 8 + 4 * (c + 1))
                sp.sem_inc(sp_passed, 1)
                sp.dma_start(out[f, c * BANK:(c + 1) * BANK, :].rearrange("(t p) d -> p t d", p=P), y[:, :, :])\
                    .then_inc(out_stored, 16)

            def one(b, f, last=False):
                store_parts(b, 0)
                store_parts(b, 1)
                stack(b, 0)
                stack(b, 1)
                store_parts(b, 2)
                store_parts(b, 3)
                max_rows(b, 0)
                if f is not None:
                    store_out(f, 0)
                load_x(b + 1) if not last else None
                if f is not None:
                    store_out(f, 1)
                for g in range(G):
                    if g + 1 < G:
                        max_rows(b, g + 1)
                    if g + 2 < G:
                        stack(b, g + 2)

            one(0, None)
            with sp.Fori(0, B - 2) as i:
                one(i + 1, i)
            one(B - 1, B - 2, last=True)
            store_out(B - 1, 0)
            store_out(B - 1, 1)
            sp.wait_ge(out_stored, B * 32 + 16)

        @block.tensor
        def _(pe):
            def turn(dst, src):
                return pe.matmul(dst, src, id_sb[:, :], start=True, stop=True, is_transpose=True,
                                 skip_group_check=True)

            def project(b):
                if b is None:
                    b = 0
                    pe.wait_ge(consts_in, 16 * 11)
                    pe.wait_ge(ready, 1)
                else:
                    pe.wait_ge(at_copied, b * 2)
                pe.wait_ge(x_loaded, b * 16 + 16)
                for h in range(2):
                    for c in range(NC):
                        for t in range(4):
                            mm = turn(psum[:, 2 * h + c, t * P:(t + 1) * P],
                                      x_in[:, 4 * h + t, c * P:(c + 1) * P])
                    mm.then_inc(xt_mm, 1)
                if not isinstance(b, int):
                    pe.wait_ge(res_done, b * T)
                for h in range(2):
                    pe.wait_ge(xt_copied, b * 2 + h + 1)
                    for t in range(4 * h, 4 * h + 4):
                        for c in range(NC):
                            mm = pe.matmul(psum[:, 4 + t // 2, (t % 2) * D:(t % 2 + 1) * D],
                                           x_t[:, c, t * P:(t + 1) * P], w_qkv[:, c, 0, :],
                                           start=(c == 0), stop=(c == NC - 1), skip_group_check=True)
                    mm.then_inc(v_mm, 1)
                for n in range(4):
                    if n >= 2:
                        pe.wait_ge(v_copied, b * 2 + n - 1)
                    for h in range(2):
                        for c in range(NC):
                            mm = pe.matmul(psum[:, 2 * n + h, :],
                                           w_qkv[:, c, 1 + n % 2, (n // 2) * P:(n // 2 + 1) * P],
                                           x_t[:, c, h * BANK:(h + 1) * BANK],
                                           start=(c == 0), stop=(c == NC - 1), skip_group_check=True)
                    mm.then_inc(qk_mm, 1)

            def turn_x1(b, f):
                if b is not None:
                    pe.wait_ge(cos_done, b * 4 + 2)
                pe.wait_ge(x1_done, f * T + T)
                if b is None:
                    pe.wait_ge(at_copied, f * 2 + 2)
                for h in range(2):
                    for c in range(NC):
                        for t in range(4):
                            mm = turn(psum[:, 2 * h + c, t * P:(t + 1) * P], x1[:, 4 * h + t, c * P:(c + 1) * P])
                    mm.then_inc(x1t_mm, 1)

            def mlp(f, k):
                n = 0

                def bank():
                    nonlocal n
                    if n < 4:
                        if k == 0:
                            pe.wait_ge(x1_lo_done, f * 2 + 2)
                        else:
                            pe.wait_ge(y_done, f * 8 + n + 1)
                    elif n < 20:
                        pe.wait_ge(h_lo, f * 32 + 16 * k + n - 3)
                    n += 1
                    return (n - 1) % 4

                for o in range(F // P):
                    q = bank()
                    for c in range(NC):
                        for a in (x1_hi, x1_lo):
                            mm = pe.matmul(psum[:, q, :], w0[:, c, o * P:(o + 1) * P],
                                           a[:, c, k * BANK:(k + 1) * BANK],
                                           start=(c == 0 and a is x1_hi), stop=(c == NC - 1 and a is x1_lo),
                                           skip_group_check=True)
                    mm.then_inc(ff_mm, 1)
                pe.wait_ge(h_lo, f * 32 + 16 * k + 8)
                for o in range(F // P):
                    q = bank()
                    for c in range(F // P):
                        for i, a in enumerate(h1):
                            mm = pe.matmul(psum[:, q, :], w1[:, c, o * P:(o + 1) * P], a[:, c, :],
                                           start=(c == 0 and i == 0), stop=(c == 7 and i == 1),
                                           skip_group_check=True)
                    mm.then_inc(ff_mm, 1)
                pe.wait_ge(h_lo, f * 32 + 16 * k + 16)
                for t in range(4):
                    q = bank()
                    for c in range(F // P):
                        for i, a in enumerate(h2):
                            mm = pe.matmul(psum[:, q, 0:D], a[:, c, t * P:(t + 1) * P], w2[:, c, :],
                                           start=(c == 0 and i == 0), stop=(c == 7 and i == 1),
                                           skip_group_check=True)
                    mm.then_inc(ff_mm, 1)

            def maxima(b, g, lo, hi):
                for n in range(lo, hi):
                    j, u = divmod(n, NMX)
                    if n == 0:
                        pe.wait_ge(stacked[g % 2], b * 384 + 192 * (g // 2) + 192)
                        if g == 0:
                            pe.wait_ge(cos_done, b * 4 + 3)
                        else:
                            pe.wait_ge(m_taken, b * 4 + g)
                    if g or n >= 2:
                        pe.wait_ge(mx_read, b * G * MXG + g * MXG + n - 1)
                    for t, a, e, col in MX_UNITS[u]:
                        mm = pe.matmul(psum[:, 4 + n % 2, col:col + e - a],
                                       q_st[0:KR, g % 2, j, t * P:(t + 1) * P], k_st[0:KR, g % 2, j, a:e],
                                       start=True, stop=True, skip_group_check=True)
                    mm.then_inc(mx_mm, 1)

            def turn_maxima(b, g):
                pe.wait_ge(m_found, b * 4 + g + 1)
                turn(psum[:, 4, 0:P], m_col[:, :]).then_inc(m_mm, 1)

            def ring_wait(b, f, use):
                i = SLOT[use]
                if i < 2:
                    if f is not None:
                        pe.wait_ge(y_done, f * 8 + 8)
                    else:
                        pe.wait_ge(cos_done, b * 4 + 2)
                else:
                    kind, g, u, h = ST_RING[i - 2]
                    if kind == "st":
                        pe.wait_ge(exp_done, b * 72 + 18 * g + 2 * u + h + 1)
                    else:
                        pe.wait_ge(normed, b * 4 + g + 1)
                return 2 * (i % 2)

            def scores_t(b, f, g, u):
                if u == 0:
                    pe.wait_ge(m_rows, b * 192 + 48 * (g + 1))
                for h in range(2):
                    q = ring_wait(b, f, ("st", g, u, h))
                    for i in range(2):
                        for t, a, e, col in ST_UNITS[u]:
                            mm = pe.matmul(psum[:, q + i, col:col + e - a],
                                           k_st[0:KM, g % 2, 2 * h + i, t * P:(t + 1) * P],
                                           q_st[0:KM, g % 2, 2 * h + i, a:e],
                                           start=True, stop=True, skip_group_check=True)
                    mm.then_inc(st_mm, 1)

            def times_v(b, g, u):
                if u == 0:
                    if g == 0:
                        pe.wait_ge(cos_done, b * 4 + 4)
                    else:
                        pe.wait_ge(o_copied, b * 4 + g)
                pe.wait_ge(exp_done, b * 72 + 18 * g + 2 * u + 2)
                if u in MASKED:
                    pe.wait_ge(mask_done, b * 4 * NMASK + NMASK * g + MASKED.index(u) + 1)
                for t, a, e, col in ST_UNITS[u]:
                    bank, first = a // BANK, a - a // BANK * BANK
                    for j in range(HG):
                        mm = pe.matmul(psum[32 * j:32 * j + 32, 6 + bank, first:first + e - a],
                                       v_ones[:, t, HG * g + j, :],
                                       probs[:, (NU * g + u) % RING, j, col:col + e - a],
                                       start=(t == 0), stop=(u == NU - 1 or (bank == 0 and u == 4)),
                                       skip_group_check=True)
                mm.then_inc(pv_done, 1)

            def turn_o(b, f, g):
                pe.wait_ge(o_copied, b * 4 + g + 1)
                q = ring_wait(b, f, ("ot", g, 0, 0))
                for t in range(T):
                    mm = turn(psum[:, q + t // 4, (t % 4) * P:(t % 4 + 1) * P], o_t[:, t * P:(t + 1) * P])
                mm.then_inc(ot_mm, 1)

            def attention(b, f):
                for g in range(G):
                    n = 0
                    for u in range(NU):
                        scores_t(b, f, g, u)
                        if g + 1 < G:
                            maxima(b, g + 1, n, n + MX_AT[u])
                            n += MX_AT[u]
                        if u == 3 and g > 0:
                            turn_o(b, f, g - 1)
                        if u == NU - 1 and g + 1 < G:
                            turn_maxima(b, g + 1)
                        if u >= LAG:
                            times_v(b, g, u - LAG)
                        elif g > 0:
                            times_v(b, g - 1, NU - LAG + u)
                for u in range(NU - LAG, NU):
                    times_v(b, G - 1, u)
                turn_o(b, f, G - 1)

            def out_project(b):
                pe.wait_ge(normed, b * 4 + 4)
                for c in range(NC):
                    if c == 0:
                        pe.wait_ge(exp_done, b * 72 + 72)
                    for t in range(T):
                        mm = turn(psum[:, 2 * c + t // 4, (t % 4) * P:(t % 4 + 1) * P],
                                  attn[:, t, c * P:(c + 1) * P])
                    mm.then_inc(at_mm, 1)
                pe.wait_ge(at_copied, b * 2 + 2)
                pe.wait_ge(m_taken, b * 4 + 4)
                pe.wait_ge(o_copied, b * 4 + 4)
                for t in range(T):
                    for c in range(NC):
                        mm = pe.matmul(psum[:, 4 + t // 2, (t % 2) * D:(t % 2 + 1) * D],
                                       attn_t[:, c, t * P:(t + 1) * P], w_o[:, c, :],
                                       start=(c == 0), stop=(c == NC - 1), skip_group_check=True)
                    mm.then_inc(wo_mm, 1)

            def one(b, f):
                project(b if f is not None else None)
                if f is not None:
                    turn_x1(b, f)
                    mlp(f, 0)
                else:
                    pass
                maxima(b, 0, 0, MXG)
                turn_maxima(b, 0)
                if f is not None:
                    mlp(f, 1)
                attention(b, f)
                out_project(b)

            one(0, None)
            with pe.Fori(0, B - 1) as i:
                one(i + 1, i)
            turn_x1(None, B - 1)
            mlp(B - 1, 0)
            mlp(B - 1, 1)

        @block.scalar
        def _(act):
            def project(b):
                for h in range(2):
                    act.wait_ge(xt_mm, b * 2 + h + 1)
                    act.activation(x_t[:, :, h * BANK:(h + 1) * BANK], psum[:, 2 * h:2 * h + 2, :], ACT.Copy)\
                        .then_inc(xt_copied, 1)
                for h in range(2):
                    act.wait_ge(v_mm, b * 2 + h + 1)
                    act.activation(v_ones[:, 4 * h:4 * h + 4, :, 0:HD],
                                   psum[:, 4 + 2 * h:6 + 2 * h, :].rearrange("p b (t h d) -> p (b t) h d", t=2, d=HD),
                                   ACT.Copy).then_inc(v_copied, 1)

            def turn_x1(f):
                for h in range(2):
                    act.wait_ge(x1t_mm, f * 2 + h + 1)
                    act.activation(x1_hi[:, :, h * BANK:(h + 1) * BANK], psum[:, 2 * h:2 * h + 2, :], ACT.Copy)\
                        .then_inc(x1_hi_done, 1)

            def mlp(f, k):
                for n in range(16):
                    act.wait_ge(ff_mm, f * 40 + 20 * k + n + 1)
                    h = (h1 if n < 8 else h2)[0]
                    act.activation(h[:, n % 8, :], psum[:, n % 4, :], ACT.Relu).then_inc(h_hi, 1)

            def exps(b, g, u, h):
                act.wait_ge(st_mm, b * 72 + 18 * g + 2 * u + h + 1)
                U = NU * g + u
                if U >= RING and h == 0:
                    act.wait_ge(pv_done, b * 36 + U - RING + 1)
                q = 2 * (SLOT[("st", g, u, h)] % 2)
                act.activation(probs[:, U % RING, 2 * h:2 * h + 2, :], psum[:, q:q + 2, :], ACT.Exp,
                               scale=SCALE).then_inc(exp_done, 1)

            def copy_o(b, g):
                act.wait_ge(pv_done, b * 36 + NU * (g + 1))
                if g > 0:
                    act.wait_ge(ot_mm, b * 4 + g)
                act.activation(o_t[:, :], psum[:, 6:8, :], ACT.Copy).then_inc(o_copied, 1)

            def attention(b):
                for g in range(G):
                    for u in range(NU):
                        exps(b, g, u, 0)
                        if u == LAG and g > 0:
                            copy_o(b, g - 1)
                        exps(b, g, u, 1)
                copy_o(b, G - 1)
                for c in range(NC):
                    act.wait_ge(at_mm, b * 2 + c + 1)
                    act.activation(attn_t[:, c, :], psum[:, 2 * c:2 * c + 2, :], ACT.Copy).then_inc(at_copied, 1)

            def one(b, f):
                project(b)
                if f is not None:
                    turn_x1(f)
                    mlp(f, 0)
                    mlp(f, 1)
                attention(b)

            act.wait_ge(pool_ready, 1)
            act.wait_ge(ready, 2)
            one(0, None)
            with act.Fori(0, B - 1) as i:
                one(i + 1, i)
            turn_x1(B - 1)
            mlp(B - 1, 0)
            mlp(B - 1, 1)

        @block.gpsimd
        def _(pool):
            pool.memset(v_ones[:, :, :, HD + 1:32], 0.0)
            pool.memset(v_ones[:, :, :, HD:HD + 1], 1.0).then_inc(pool_ready, 1)

            def keep_x(b):
                pool.wait_ge(x_loaded, b * 16 + 16)
                if not isinstance(b, int):
                    pool.wait_ge(res_done, b * T)
                pool.sem_inc(pool_passed, 1)
                pool.tensor_copy(x_res[:, :, :], x_in[:, :, :]).then_inc(x_kept, 1)

            def times_sin(b, n):
                pool.wait_ge(swap_done, b * 4 + n + 1)
                if n or not isinstance(b, int):
                    pool.wait_ge(parts_done, b * 4 + n)
                pool.tensor_tensor(rest, swapped, sin_sb[:, :], ALU.mult).then_inc(sin_done, 1)

            def inv_std(done, eps_ready, n, dst, src, width):
                pool.wait_ge(eps_ready, n)
                pool.tensor_tensor(dst, src, minus_half[:, 0:width], ALU.pow).then_inc(done, 1)

            def masks(b, g):
                for i, u in enumerate(MASKED):
                    pool.wait_ge(exp_done, b * 72 + 18 * g + 2 * u + 2)
                    pool.sem_inc(pool_passed, 1)
                    for col in DIAG[u]:
                        blk = probs[:, (NU * g + u) % RING, :, col:col + P]
                        op = pool.affine_select(out=blk, in_=blk, compare_op=ALU.is_ge, fill=0.0, base=0,
                                                pattern=[[0, HG], [1, P]], channel_multiplier=-1)
                    op.then_inc(mask_done, 1)

            def one(b, f):
                keep_x(b)
                for n in range(4):
                    times_sin(b, n)
                if f is not None:
                    inv_std(rstd2_done, eps2_done, f * 2 + 1, rstd2[:, :], var_eps2[:, :], 4)
                    inv_std(rstd2_done, eps2_done, f * 2 + 2, rstd2[:, :], var_eps2[:, :], 4)
                for g in range(G):
                    masks(b, g)
                inv_std(rstd_done, eps_done, b + 1, rstd[:, :], var_eps[:, :], T)

            pool.wait_ge(ready, 1)
            pool.wait_ge(consts_in, 16 * 11)
            one(0, None)
            with pool.Fori(0, B - 1) as i:
                one(i + 1, i)
            inv_std(rstd2_done, eps2_done, (B - 1) * 2 + 1, rstd2[:, :], var_eps2[:, :], 4)
            inv_std(rstd2_done, eps2_done, (B - 1) * 2 + 2, rstd2[:, :], var_eps2[:, :], 4)

        @block.vector
        def _(dve):
            dumps = [0]
            SWAP = [i ^ 1 for i in range(32)]

            def rope(b, n):
                ps = psum[:, 2 * n:2 * n + 2, :].rearrange("p b n -> p (b n)")
                if n == 0 and not isinstance(b, int):
                    dve.wait_ge(wo_mm, b * T)
                dve.wait_ge(qk_mm, b * 4 + n + 1)
                dve.sem_inc(dve_passed, 1)
                dve.stream_shuffle(swapped, ps, SWAP).then_inc(swap_done, 1)
                yield
                if n or not isinstance(b, int):
                    dve.wait_ge(parts_done, b * 4 + n)
                dve.tensor_tensor(turned, ps, cos_sb[:, :], ALU.mult).then_inc(cos_done, 1)
                yield
                dve.wait_ge(cos_done, b * 4 + n + 1)
                dve.wait_ge(sin_done, b * 4 + n + 1)
                dve.tensor_tensor(turned, turned, rest, ALU.add).then_inc(turned_done, 1)
                yield
                if n >= 2 or not isinstance(b, int):
                    dve.wait_ge(stored[n % 2], b * 32 + (n // 2) * 16)
                dve.wait_ge(turned_done, b * 4 + n + 1)
                dve.tensor_copy(parts[:, n % 2, 0, :], turned).then_inc(hi_done, 1)
                yield
                dve.wait_ge(hi_done, b * 4 + n + 1)
                dve.tensor_tensor(rest, turned, parts[:, n % 2, 0, :], ALU.subtract).then_inc(rest_done, 1)
                yield
                dve.wait_ge(rest_done, b * 4 + n + 1)
                dve.tensor_copy(parts[:, n % 2, 1, :], rest).then_inc(mid_done, 1)
                yield
                dve.wait_ge(mid_done, b * 4 + n + 1)
                dve.tensor_tensor(parts[:, n % 2, 2, :], rest, parts[:, n % 2, 1, :], ALU.subtract)\
                    .then_inc(parts_done, 1)
                yield

            def turn_x1(f):
                for h in range(2):
                    dve.wait_ge(x1_hi_done, f * 2 + h + 1)
                    dve.tensor_tensor(x1_lo[:, :, h * BANK:(h + 1) * BANK], psum[:, 2 * h:2 * h + 2, :],
                                      x1_hi[:, :, h * BANK:(h + 1) * BANK], ALU.subtract).then_inc(x1_lo_done, 1)

            def mlp(f, k, beside=None):
                for n in range(16):
                    h = h1 if n < 8 else h2
                    dve.wait_ge(h_hi, f * 32 + 16 * k + n + 1)
                    dve.scalar_tensor_tensor(out=h[1][:, n % 8, :], in0=psum[:, n % 4, :], scalar=0.0,
                                             in1=h[0][:, n % 8, :], op0=ALU.max, op1=ALU.subtract)\
                        .then_inc(h_lo, 1)
                    if beside is not None and n >= 8:
                        next(beside, None)
                        next(beside, None)
                if k == 0:
                    dve.wait_ge(out_stored, f * 32 + 16)
                else:
                    dve.wait_ge(out_stored, f * 32 + 32)
                for t in range(4):
                    dve.wait_ge(ff_mm, f * 40 + 20 * k + 17 + t)
                    dve.scalar_tensor_tensor(out=y[:, t, :], in0=psum[:, t, 0:D], scalar=factor[:, 0:1],
                                             in1=x1[:, 4 * k + t, :], op0=ALU.mult, op1=ALU.add)\
                        .then_inc(y_done, 1)
                for t in range(4):
                    dve.wait_ge(y_done, f * 8 + 4 * k + t + 1)
                    dve.bn_stats(stats2[:, t, :], y[:, t, :]).then_inc(stat2_done, 1)
                for t in range(4):
                    dve.wait_ge(stat2_done, f * 8 + 4 * k + t + 1)
                    dve.sem_inc(dve_passed, 1)
                    dve.bn_aggr(mean_var2[:, t, :], stats2[:, t, :]).then_inc(aggr2_done, 1)
                dve.wait_ge(aggr2_done, f * 8 + 4 * k + 4)
                dve.tensor_scalar(var_eps2[:, :], mean_var2[:, :, 1], EPS, None, ALU.add).then_inc(eps2_done, 1)

            def finish(f, k):
                dve.wait_ge(rstd2_done, f * 2 + k + 1)
                for t in range(4):
                    dve.tensor_scalar(y[:, t, :], y[:, t, :], mean_var2[:, t, 0:1], rstd2[:, t:t + 1],
                                      ALU.subtract, ALU.mult).then_inc(out_done, 1)

            def maxima(b, g, lo, hi):
                for n in range(lo, hi):
                    j, u = divmod(n, NMX)
                    if n == 0:
                        if g >= 2:
                            dve.wait_ge(m_found, b * 4 + g - 1)
                        elif not isinstance(b, int):
                            dve.wait_ge(m_found, b * 4 + g - 1)
                    dve.wait_ge(mx_mm, b * G * MXG + g * MXG + n + 1)
                    for t, a, e, col in MX_UNITS[u]:
                        diag = e == (t + 1) * P
                        wide = e - a - (P if diag else 0)
                        if wide:
                            op = dve.tensor_reduce(mx[:, g % 2, j, t, a // BANK:a // BANK + 1],
                                                   psum[:, 4 + n % 2, col:col + wide], AX.X, ALU.max)
                        if diag:
                            dumps[0] += 1
                            op = dve.tensor_tensor_reduce(dump[:, dumps[0] % 4, :], psum[:, 4 + n % 2, col + wide:col + wide + P],
                                                          tri_sb[:, :], 1.0, LOWEST, ALU.add, ALU.max,
                                                          mx[:, g % 2, j, t, 2:3])
                    op.then_inc(mx_read, 1)

            def find_maxima(b, g):
                dve.wait_ge(mx_read, b * G * MXG + (g + 1) * MXG)
                if g or not isinstance(b, int):
                    dve.wait_ge(m_mm, b * 4 + g)
                dve.tensor_reduce(m_col[:, 0:HG * T], mx[:, g % 2].rearrange("p j t a -> p (j t) a"), AX.X,
                                  ALU.max).then_inc(m_found, 1)

            def split_maxima(b, g):
                mt = psum[0:HG * T, 4, 0:P]
                dve.wait_ge(m_mm, b * 4 + g + 1)
                dve.wait_ge(m_rows, b * 192 + 48 * g)
                dve.tensor_scalar(m_parts[:, 0, :], mt, -1.0, None, ALU.mult).then_inc(m_hi, 1)
                dve.wait_ge(m_hi, b * 4 + g + 1)
                dve.scalar_tensor_tensor(out=m_rest[:, :], in0=mt, scalar=-1.0, in1=m_parts[:, 0, :],
                                         op0=ALU.mult, op1=ALU.subtract).then_inc(m_taken, 1)
                dve.wait_ge(m_taken, b * 4 + g + 1)
                dve.tensor_copy(m_parts[:, 1, :], m_rest[:, :]).then_inc(m_mid, 1)
                dve.wait_ge(m_mid, b * 4 + g + 1)
                dve.tensor_tensor(m_parts[:, 2, :], m_rest[:, :], m_parts[:, 1, :], ALU.subtract)\
                    .then_inc(m_split, 1)

            def normalise(b, g):
                q = 2 * (SLOT[("ot", g, 0, 0)] % 2)
                o = psum[:, q:q + 2, :].rearrange("p b (t j d) -> p (b t) j d", t=4, j=HG)
                dve.wait_ge(ot_mm, b * 4 + g + 1)
                if g or not isinstance(b, int):
                    dve.wait_ge(normed, b * 4 + g)
                dve.reciprocal(recip[:, :, :], o[:, :, :, HD]).then_inc(recip_done, 1)
                dve.wait_ge(recip_done, b * 4 + g + 1)
                if g == 0 and not isinstance(b, int):
                    dve.wait_ge(at_mm, b * 2)
                dst = attn[:, :, HG * HD * g:HG * HD * (g + 1)].rearrange("p t (j d) -> p t j d", j=HG)
                dve.tensor_tensor(dst, o[:, :, :, 0:HD],
                                  recip[:, :, :].unsqueeze(3).to_broadcast([P, T, HG, HD]), ALU.mult)\
                    .then_inc(normed, 1)

            def attention(b):
                for g in range(G):
                    n = 0
                    for u in range(NU):
                        if g + 1 < G:
                            maxima(b, g + 1, n, n + MX_AT[u])
                            n += MX_AT[u]
                            if n == MXG and MX_AT[u]:
                                find_maxima(b, g + 1)
                        if u == 3 and g > 0:
                            normalise(b, g - 1)
                        if u == NU - 1 and g + 1 < G:
                            split_maxima(b, g + 1)
                normalise(b, G - 1)

            def norm1(b):
                for t in range(T):
                    dve.wait_ge(wo_mm, b * T + t // 2 * 2 + 2)
                    if t == 0:
                        dve.wait_ge(x_kept, b + 1)
                        if not isinstance(b, int):
                            dve.wait_ge(y_done, b * 8)
                            dve.wait_ge(x1t_mm, b * 2)
                    dve.tensor_tensor(x1[:, t, :], psum[:, 4 + t // 2, (t % 2) * D:(t % 2 + 1) * D],
                                      x_res[:, t, :], ALU.add).then_inc(res_done, 1)
                for t in range(T):
                    dve.wait_ge(res_done, b * T + t + 1)
                    dve.bn_stats(stats[:, t, :], x1[:, t, :]).then_inc(stat_done, 1)
                for t in range(T):
                    dve.wait_ge(stat_done, b * T + t + 1)
                    dve.sem_inc(dve_passed, 1)
                    dve.bn_aggr(mean_var[:, t, :], stats[:, t, :]).then_inc(aggr_done, 1)
                dve.wait_ge(aggr_done, b * T + T)
                dve.tensor_scalar(var_eps[:, :], mean_var[:, :, 1], EPS, None, ALU.add).then_inc(eps_done, 1)
                dve.wait_ge(rstd_done, b + 1)
                for t in range(T):
                    dve.tensor_scalar(x1[:, t, :], x1[:, t, :], mean_var[:, t, 0:1], rstd[:, t:t + 1],
                                      ALU.subtract, ALU.mult).then_inc(x1_done, 1)

            def run(gen):
                for _ in gen:
                    pass

            def chain(*gens):
                for gen in gens:
                    yield from gen

            def one(b, f):
                run(rope(b, 0))
                run(rope(b, 1))
                if f is not None:
                    turn_x1(f)
                    late = chain(rope(b, 2), rope(b, 3))
                    mlp(f, 0, late)
                    run(late)
                else:
                    run(rope(b, 2))
                    run(rope(b, 3))
                maxima(b, 0, 0, MXG)
                find_maxima(b, 0)
                split_maxima(b, 0)
                if f is not None:
                    finish(f, 0)
                    mlp(f, 1)
                    finish(f, 1)
                attention(b)
                norm1(b)

            dve.memset(m_col[:, :], 0.0)
            dve.memset(k_st[96:128, :, :, :], 1.0)
            dve.memset(minus_half[:, :], -0.5)
            dve.memset(mx[:, :, :, :, :], LOWEST).then_inc(ready, 1)
            dve.wait_ge(w_in, 16 * 6)
            step = sem("setup_step")
            dve.tensor_scalar(s_sign[:, :], s_in[:, :], 0.0, 2.0, ALU.is_ge, ALU.mult).then_inc(step, 1)
            dve.wait_ge(step, 1)
            dve.tensor_scalar(s_sign[:, :], s_sign[:, :], -1.0, None, ALU.add).then_inc(step, 1)
            dve.wait_ge(step, 2)
            dve.tensor_tensor(s_abs[:, :], s_in[:, :], s_sign[:, :], ALU.mult).then_inc(step, 1)
            dve.wait_ge(step, 3)
            dve.tensor_tensor(s_prod[:, :], s_abs[:, 0:1], s_abs[:, 1:2], ALU.mult).then_inc(step, 1)
            dve.wait_ge(step, 4)
            dve.scalar_tensor_tensor(out=factor[:, :], in0=s_prod[:, :], scalar=OUT_FACTOR, in1=s_in[:, 2:3],
                                     op0=ALU.mult, op1=ALU.mult).then_inc(step, 1)
            dve.tensor_tensor(w0[:, :, :], k0_u8[:, 0:2, :], k0_u8[:, 2:4, :], ALU.subtract).then_inc(step, 1)
            dve.tensor_scalar(w1[:, :, :], k1_u8, 2.0 * W1_SCALE, -W1_SCALE, ALU.mult, ALU.add).then_inc(step, 1)
            dve.tensor_scalar(w2[:, :, :], k2_u8, 2.0, -1.0, ALU.mult, ALU.add).then_inc(step, 1)
            dve.wait_ge(step, 8)
            dve.tensor_scalar(w0[:, :, :], w0[:, :, :], s_sign[:, 0:1], None, ALU.mult).then_inc(step, 1)
            dve.tensor_scalar(w1[:, :, :], w1[:, :, :], s_sign[:, 1:2], None, ALU.mult).then_inc(ready, 1)
            dve.wait_ge(pool_ready, 1)
            dve.wait_ge(consts_in, 16 * 11)

            one(0, None)
            with dve.Fori(0, B - 1) as i:
                one(i + 1, i)
            turn_x1(B - 1)
            mlp(B - 1, 0)
            finish(B - 1, 0)
            mlp(B - 1, 1)
            finish(B - 1, 1)


NAMES = ("x", "wq", "wk", "wv", "wo", "k0", "k1", "k2", "s0", "s1", "s2")


def rope_tables():
    inv = (np.float32(1.0) / np.float32(10000.0) ** (np.arange(0, HD, 2, dtype=np.float32) / np.float32(HD)))
    ang = (np.arange(S, dtype=np.float32)[None, :] * inv.astype(np.float32)[:, None]).astype(np.float32)
    row = np.arange(P) % HD
    a = ang[row // 2]
    sign = np.where(row % 2 == 0, -1.0, 1.0)[:, None]
    return np.cos(a.astype(np.float64)).astype(np.float32), (np.sin(a.astype(np.float64)) * sign).astype(np.float32)


def kernel(L0_attn_x, L0_attn_wq, L0_attn_wk, L0_attn_wv, L0_attn_wo, L0_ffn_k0, L0_ffn_k1, L0_ffn_k2,
           L0_ffn_s0, L0_ffn_s1, L0_ffn_s2):
    import concourse.bacc as bacc
    from concourse.bass_utils import run_bass_kernel_spmd

    cos, sin = rope_tables()
    row, col = np.arange(P)[:, None], np.arange(P)[None, :]
    arrays = {
        "x": np.ascontiguousarray(L0_attn_x),
        "wq": np.ascontiguousarray(L0_attn_wq),
        "wk": np.ascontiguousarray(L0_attn_wk),
        "wv": np.ascontiguousarray(L0_attn_wv),
        "wo": np.ascontiguousarray(L0_attn_wo),
        "k0": np.ascontiguousarray(L0_ffn_k0),
        "k1": np.ascontiguousarray(L0_ffn_k1),
        "k2": np.ascontiguousarray(L0_ffn_k2),
        "s0": np.asarray(L0_ffn_s0).reshape(1),
        "s1": np.asarray(L0_ffn_s1).reshape(1),
        "s2": np.asarray(L0_ffn_s2).reshape(1),
        "cos": cos,
        "sin": sin,
        "ident": np.eye(P, dtype=np.float32),
        "tri": np.where(col <= row, 0.0, -1.0e38).astype(np.float32),
    }
    nc = bacc.Bacc("TRN2", target_bir_lowering=False, num_devices=1)
    ins = [nc.dram_tensor(f"in_{n}", a.shape, mybir.dt.from_np(a.dtype), kind="ExternalInput").ap()
           for n, a in arrays.items()]
    out = nc.dram_tensor("out", (B, S, D), F32, kind="ExternalOutput").ap()
    scratch = nc.dram_tensor("scratch", (2, 2, 3, P, S), BF16).ap()
    build(nc, *ins, out, scratch)
    r = run_bass_kernel_spmd(nc, [{f"in_{n}": a for n, a in arrays.items()}], core_ids=[0])
    return r.results[0]["out"]
```

```python
from contextlib import ExitStack

import concourse.bass as bass
from concourse import mybir
import numpy as np

F32, BF16, F16, U8 = mybir.dt.float32, mybir.dt.bfloat16, mybir.dt.float16, mybir.dt.uint8
ALU, ACT, AX = mybir.AluOpType, mybir.ActivationFunctionType, mybir.AxisListType

P = 128
B, S, D = 8, 1024, 256
H, HD = 16, 16
T = S // P
F = 1024
HG = 4
G = H // HG
NC = D // P
BANK = 512
EPS = 1e-5
LOWEST = -3.0e38
SCALE = float(HD) ** -0.5
Q_PARTS = (0, 1, 2, 0, 1, 0)
K_PARTS = (0, 0, 0, 1, 1, 2)
KR = HD * len(Q_PARTS)
KM = KR + 3
W1_SCALE = 1.0 / 16
OUT_FACTOR = 2.0 * 2.0 * 2.0 / W1_SCALE

def spread(n, i, of):
    return n * (i + 1) // of - n * i // of


ST_UNITS = (
    ((0, 0, 512, 0),),
    ((0, 512, 1024, 0),),
    ((1, 128, 512, 0), (7, 896, 1024, 384)),
    ((2, 256, 512, 0), (6, 768, 1024, 256)),
    ((3, 384, 512, 0), (5, 640, 1024, 128)),
    ((4, 512, 1024, 0),),
    ((1, 512, 1024, 0),),
    ((2, 512, 1024, 0),),
    ((3, 512, 1024, 0),),
)
NU = len(ST_UNITS)
DIAG = tuple(tuple(c for k, a, b, c in u if a == k * P) for u in ST_UNITS)
MASKED = tuple(u for u in range(NU) if DIAG[u])
MX_UNITS = (
    ((7, 0, 512, 0),),
    ((7, 512, 1024, 0),),
    ((6, 0, 512, 0),),
    ((6, 512, 896, 0), (0, 0, 128, 384)),
    ((5, 0, 512, 0),),
    ((5, 512, 768, 0), (1, 0, 256, 256)),
    ((4, 0, 512, 0),),
    ((3, 0, 512, 0),),
    ((2, 0, 384, 0), (4, 512, 640, 384)),
)
NMX = len(MX_UNITS)
MX_STEPS = HG * NMX + 1
ROPE_BESIDE = (3, 3, 3, 3, 2, 0, 0, 0)
MX_BESIDE = ((0, 0, 0, 0, 0, 4, 4, 4, 2, 2, 2, 2), (5, 5, 5, 5, 5, 5, 5, 5, 2, 2, 2, 2))
MX_MLP = sum(map(sum, MX_BESIDE))
MX_SLOTS = (G - 1) * NU - 2
MX_AT = tuple(spread(G * MX_STEPS - MX_MLP, i, MX_SLOTS) if i < MX_SLOTS else 0 for i in range(G * NU))
assert MX_MLP + sum(MX_AT) == G * MX_STEPS and not any(MX_AT[-NU:])
STACK_OF = (0, 1, 2, 0)
V_ROW = HD + 1
LAG = 2
RING = 3


def st_ring():
    uses = []
    for g in range(G):
        for u in range(NU):
            uses += [("st", g, u, 0), ("st", g, u, 1)]
            if u == 3 and g > 0:
                uses.append(("ot", g - 1, 0, 0))
    uses.append(("ot", G - 1, 0, 0))
    return uses


ST_RING = st_ring()
SLOT = {use: i for i, use in enumerate(ST_RING)}


def take(steps, n):
    if steps is not None:
        for _ in range(n):
            next(steps, None)


def first(b):
    return isinstance(b, int) and b == 0


def build(nc, x, wq, wk, wv, wo, k0, k1, k2, s0, s1, s2, cos, sin, ident, tri, out, scratch):
    with ExitStack() as ctx:
        def sb(name, shape, dt):
            return ctx.enter_context(nc.sbuf_tensor(name, shape, dt))

        def sem(name):
            return ctx.enter_context(nc.semaphore(name))

        psum = ctx.enter_context(nc.psum_tensor("psum", [P, 8, BANK], F32))

        w_qkv = sb("w_qkv", [P, NC, 3, D], F32)
        w_o = sb("w_o", [P, NC, D], F32)
        w0 = sb("w0", [P, NC, F], F16)
        w1 = sb("w1", [P, F // P, F], F16)
        w2 = sb("w2", [P, F // P, D], F16)
        cos_sb = sb("cos_sb", [P, S], F32)
        sin_sb = sb("sin_sb", [P, S], F32)
        id_sb = sb("id_sb", [P, P], F32)
        tri_sb = sb("tri_sb", [P, P], F32)
        s_in = sb("s_in", [P, 3], F32)
        s_sign = sb("s_sign", [P, 3], F32)
        s_abs = sb("s_abs", [P, 3], F32)
        s_prod = sb("s_prod", [P, 1], F32)
        factor = sb("factor", [P, 1], F32)
        minus_half = sb("minus_half", [P, T], F32)
        x_in = sb("x_in", [P, T, D], F32)
        x_res = sb("x_res", [P, T, D], F32)
        x1 = sb("x1", [P, T, D], F32)
        v_all = sb("v_all", [P, T, H * V_ROW + 32 - V_ROW], F32)
        v_ones = v_all[:, :, 0:H * V_ROW].rearrange("p t (h d) -> p t h d", d=V_ROW)
        parts = sb("parts", [P, 2, 3, S], BF16)
        q_st = sb("q_st", [P, 3, HG, S], BF16)
        k_st = sb("k_st", [P, 3, HG, S], BF16)
        rope_buf = sb("rope_buf", [P, 3, S], F32)
        swapped, turned, rest = rope_buf[:, 0, :], rope_buf[:, 1, :], rope_buf[:, 2, :]
        region = sb("region", [P, 8192], F32)
        probs = region[:, 0:RING * HG * BANK].rearrange("p (r j n) -> p r j n", r=RING, j=HG)
        x_t = region[:, 6144:8192].rearrange("p (c n) -> p c n", c=NC)
        halves = region[:, :].bitcast(F16).rearrange("p (a f n) -> p a f n", a=4, f=F // P)
        h1, h2 = (halves[:, 0], halves[:, 1]), (halves[:, 2], halves[:, 3])
        bits = region[:, :].bitcast(U8)
        k0_u8 = bits[:, 0:4 * F].rearrange("p (c n) -> p c n", c=4)
        k1_u8 = bits[:, 4 * F:12 * F].rearrange("p (c n) -> p c n", c=8)
        k2_u8 = bits[:, 12 * F:14 * F].rearrange("p (c n) -> p c n", c=8)
        o_t = sb("o_t", [P, S], F32)
        attn = sb("attn", [P, T, D], F32)
        attn_t = region[:, 0:NC * S].rearrange("p (c n) -> p c n", c=NC)
        x1_hi = sb("x1_hi", [P, NC, S], F16)
        x1_lo = sb("x1_lo", [P, NC, S], F16)
        y = sb("y", [P, 4, D], F32)
        recip = sb("recip", [P, T, HG], F32)
        mx = sb("mx", [P, 2, HG, T, 3], F32)
        m_col = sb("m_col", [P, P], F32)
        m_rest = sb("m_rest", [HG * T, P], F32)
        m_parts = sb("m_parts", [HG * T, 3, P], BF16)
        dump = sb("dump", [P, 4, P], BF16)
        stats = sb("stats", [P, T, 6], F32)
        mean_var = sb("mean_var", [P, T, 2], F32)
        var_eps = sb("var_eps", [P, T], F32)
        rstd = sb("rstd", [P, T], F32)
        stats2 = sb("stats2", [P, 4, 6], F32)
        mean_var2 = sb("mean_var2", [P, 4, 2], F32)
        var_eps2 = sb("var_eps2", [P, 4], F32)
        rstd2 = sb("rstd2", [P, 4], F32)

        consts_in = sem("consts_in")
        w_in = sem("w_in")
        x_loaded = sem("x_loaded")
        x_kept = sem("x_kept")
        xt_mm, xt_copied = sem("xt_mm"), sem("xt_copied")
        v_mm, v_copied = sem("v_mm"), sem("v_copied")
        qk_mm = sem("qk_mm")
        swap_done = sem("swap_done")
        cos_done = sem("cos_done")
        sin_done = sem("sin_done")
        turned_done = sem("turned_done")
        hi_done, rest_done, mid_done = sem("hi_done"), sem("rest_done"), sem("mid_done")
        parts_done = sem("parts_done")
        stored = [sem("stored0"), sem("stored1")]
        stacked = [sem("stacked0"), sem("stacked1"), sem("stacked2")]
        mx_mm, mx_read = sem("mx_mm"), sem("mx_read")
        m_found = sem("m_found")
        m_hi, m_mid, m_split = sem("m_hi"), sem("m_mid"), sem("m_split")
        m_rows = sem("m_rows")
        st_mm = sem("st_mm")
        exp_done = sem("exp_done")
        mask_done = sem("mask_done")
        pv_done = sem("pv_done")
        o_copied = sem("o_copied")
        ot_mm = sem("ot_mm")
        recip_done = sem("recip_done")
        normed = sem("normed")
        at_mm, at_copied = sem("at_mm"), sem("at_copied")
        wo_mm = sem("wo_mm")
        res_done, stat_done, aggr_done, eps_done, rstd_done, x1_done = (
            sem("res_done"), sem("stat_done"), sem("aggr_done"), sem("eps_done"), sem("rstd_done"), sem("x1_done"))
        x1t_mm, x1_hi_done, x1_lo_done = sem("x1t_mm"), sem("x1_hi_done"), sem("x1_lo_done")
        ff_mm = sem("ff_mm")
        h_hi, h_lo = sem("h_hi"), sem("h_lo")
        y_done, stat2_done, aggr2_done, eps2_done, rstd2_done, out_done = (
            sem("y_done"), sem("stat2_done"), sem("aggr2_done"), sem("eps2_done"), sem("rstd2_done"), sem("out_done"))
        out_stored = sem("out_stored")
        ready = sem("ready")
        pool_ready = sem("pool_ready")

        dve_passed, pool_passed, sp_passed = sem("dve_passed"), sem("pool_passed"), sem("sp_passed")

        NMASK = len(MASKED)
        MXB = G * MX_STEPS

        def stacked_value(b, g):
            return b * 384 + 192 * (1 + (g == 3)) if STACK_OF[g] == 0 else b * 192 + 192

        block = ctx.enter_context(nc.Block())

        @block.sync
        def _(sp):
            sp.sem_inc(out_stored, 16)
            sp.dma_start(id_sb[:, :], ident).then_inc(consts_in, 16)
            for c in range(NC):
                for n, w in enumerate((wv, wq, wk)):
                    sp.dma_start(w_qkv[:, c, n, :], w[c * P:(c + 1) * P, :]).then_inc(consts_in, 16)
            sp.dma_start(x_in[:, :, :], x[0].rearrange("(t p) d -> p t d", p=P)).then_inc(x_loaded, 16)
            sp.dma_start(cos_sb[:, :], cos).then_inc(consts_in, 16)
            sp.dma_start(sin_sb[:, :], sin).then_inc(consts_in, 16)
            sp.dma_start(tri_sb[:, :], tri).then_inc(consts_in, 16)
            sp.dma_start(w_o[:, :, :], wo.rearrange("(c p) n -> p c n", p=P)).then_inc(consts_in, 16)
            for n, s in enumerate((s0, s1, s2)):
                sp.dma_start(s_in[:, n:n + 1], s.partition_broadcast(P)).then_inc(w_in, 16)
            sp.dma_start(k0_u8, k0.rearrange("(c p) n -> p c n", p=P)).then_inc(w_in, 16)
            sp.dma_start(k1_u8, k1.rearrange("(c p) n -> p c n", p=P)).then_inc(w_in, 16)
            sp.dma_start(k2_u8, k2.rearrange("(c p) n -> p c n", p=P)).then_inc(w_in, 16)

            def store_parts(b, n):
                sp.wait_ge(parts_done, b * 4 + n + 1)
                sp.sem_inc(sp_passed, 1)
                sp.dma_start(scratch[n // 2, n % 2].rearrange("r p n -> p r n"), parts[:, n % 2, :, :])\
                    .then_inc(stored[n % 2], 16)

            def stack(b, g):
                c, row, buf = g // 2, (g % 2) * HG * HD, STACK_OF[g]
                if row == 0:
                    for qk in range(2):
                        sp.wait_ge(stored[qk], b * 32 + 16 * c + 16)
                        sp.sem_inc(sp_passed, 1)
                if g == 3:
                    sp.wait_ge(st_mm, b * 72 + 18)
                    sp.sem_inc(sp_passed, 1)
                elif not first(b):
                    sp.wait_ge(st_mm, b * 72)
                    sp.sem_inc(sp_passed, 1)
                for r in range(len(Q_PARTS)):
                    for st, qk, part in ((q_st, 0, Q_PARTS[r]), (k_st, 1, K_PARTS[r])):
                        src = scratch[c, qk, part, row:row + HG * HD, :].rearrange("(j d) n -> d j n", d=HD)
                        sp.dma_start(st[r * HD:(r + 1) * HD, buf, :, :], src).then_inc(stacked[buf], 16)

            def max_rows(b, g):
                sp.wait_ge(m_split, b * 4 + g + 1)
                sp.sem_inc(sp_passed, 1)
                for r in range(3):
                    sp.dma_start(q_st[KR + r:KR + r + 1, STACK_OF[g], :, :].rearrange("p j (t n) -> p (j t) n", n=P),
                                 m_parts[:, r, :]).then_inc(m_rows, 16)

            def load_x(nxt):
                sp.wait_ge(x_kept, nxt)
                sp.sem_inc(sp_passed, 1)
                sp.wait_ge(xt_mm, nxt * 2)
                sp.sem_inc(sp_passed, 1)
                sp.dma_start(x_in[:, :, :], x[nxt].rearrange("(t p) d -> p t d", p=P)).then_inc(x_loaded, 16)

            def store_out(f, c):
                sp.wait_ge(out_done, f * 8 + 4 * (c + 1))
                sp.sem_inc(sp_passed, 1)
                sp.dma_start(out[f, c * BANK:(c + 1) * BANK, :].rearrange("(t p) d -> p t d", p=P), y[:, :, :])\
                    .then_inc(out_stored, 16)

            def one(b, f, last=False):
                stack(b, 0)
                stack(b, 1)
                store_parts(b, 2)
                store_parts(b, 3)
                stack(b, 2)
                if not last:
                    load_x(b + 1)
                if f is not None:
                    store_out(f, 0)
                max_rows(b, 0)
                if f is not None:
                    store_out(f, 1)
                max_rows(b, 1)
                stack(b, 3)
                max_rows(b, 2)
                max_rows(b, 3)
                if not last:
                    store_parts(b + 1, 0)
                    store_parts(b + 1, 1)

            store_parts(0, 0)
            store_parts(0, 1)
            one(0, None)
            with sp.Fori(0, B - 2) as i:
                one(i + 1, i)
            one(B - 1, B - 2, last=True)
            store_out(B - 1, 0)
            store_out(B - 1, 1)
            sp.wait_ge(out_stored, B * 32 + 16)

        @block.tensor
        def _(pe):
            def turn(dst, src):
                return pe.matmul(dst, src, id_sb[:, :], start=True, stop=True, is_transpose=True,
                                 skip_group_check=True)

            def turn_x(b, h):
                if h == 0:
                    pe.wait_ge(x_loaded, b * 16 + 16)
                    if not first(b):
                        pe.wait_ge(mx_read, b * MXB)
                else:
                    pe.wait_ge(xt_copied, b * 2 + 1)
                for c in range(NC):
                    for t in range(4):
                        mm = turn(psum[:, 4 + c, t * P:(t + 1) * P], x_in[:, 4 * h + t, c * P:(c + 1) * P])
                mm.then_inc(xt_mm, 1)

            def project_v(b, h):
                if h:
                    pe.wait_ge(v_copied, b * 2 + 1)
                elif first(b):
                    pe.wait_ge(xt_copied, 2)
                else:
                    pe.wait_ge(exp_done, b * 72)
                for t in range(4 * h, 4 * h + 4):
                    for c in range(NC):
                        mm = pe.matmul(psum[:, t // 2 - 2 * h, (t % 2) * D:(t % 2 + 1) * D],
                                       x_t[:, c, t * P:(t + 1) * P], w_qkv[:, c, 0, :],
                                       start=(c == 0), stop=(c == NC - 1), skip_group_check=True)
                mm.then_inc(v_mm, 1)

            def project_qk(b, n, h):
                bank = 6 if n == 3 else 4
                if h == 0:
                    if n == 0:
                        pe.wait_ge(xt_copied, b * 2 + 2)
                    elif n == 1:
                        pe.wait_ge(cos_done, b * 4 + 1)
                    elif first(b):
                        pe.wait_ge(cos_done, 2)
                    else:
                        pe.wait_ge(res_done, b * T - (4 if n == 2 else 0))
                for c in range(NC):
                    mm = pe.matmul(psum[:, bank + h, :],
                                   w_qkv[:, c, 1 + n % 2, (n // 2) * P:(n // 2 + 1) * P],
                                   x_t[:, c, h * BANK:(h + 1) * BANK],
                                   start=(c == 0), stop=(c == NC - 1), skip_group_check=True)
                if h:
                    mm.then_inc(qk_mm, 1)

            def turn_x1(f):
                pe.wait_ge(at_copied, f * 2 + 2)
                for h in range(2):
                    pe.wait_ge(x1_done, f * T + 4 * h + 4)
                    for c in range(NC):
                        for t in range(4):
                            mm = turn(psum[:, 2 * h + c, t * P:(t + 1) * P], x1[:, 4 * h + t, c * P:(c + 1) * P])
                    mm.then_inc(x1t_mm, 1)

            def mlp(f, k, steps=None):
                n = 0

                def bank():
                    nonlocal n
                    if n < 4:
                        if k == 0:
                            pe.wait_ge(x1_lo_done, f * 2 + 1 + n // 2)
                        else:
                            pe.wait_ge(y_done, f * 8 + n + 1)
                    elif n < 20:
                        pe.wait_ge(h_lo, f * 32 + 16 * k + n - 3)
                    n += 1
                    return (n - 1) % 4

                for o in range(F // P):
                    q = bank()
                    for c in range(NC):
                        for a in (x1_hi, x1_lo):
                            mm = pe.matmul(psum[:, q, :], w0[:, c, o * P:(o + 1) * P],
                                           a[:, c, k * BANK:(k + 1) * BANK],
                                           start=(c == 0 and a is x1_hi), stop=(c == NC - 1 and a is x1_lo),
                                           skip_group_check=True)
                    mm.then_inc(ff_mm, 1)
                for o in range(F // P):
                    q = bank()
                    for c in range(F // P):
                        if o == 0:
                            pe.wait_ge(h_lo, f * 32 + 16 * k + c + 1)
                        for i, a in enumerate(h1):
                            mm = pe.matmul(psum[:, q, :], w1[:, c, o * P:(o + 1) * P], a[:, c, :],
                                           start=(c == 0 and i == 0), stop=(c == 7 and i == 1),
                                           skip_group_check=True)
                        if c == 7:
                            mm.then_inc(ff_mm, 1)
                        take(steps, spread(MX_BESIDE[k][o], c, 8))
                for t in range(4):
                    q = bank()
                    for c in range(F // P):
                        if t == 0:
                            pe.wait_ge(h_lo, f * 32 + 16 * k + 8 + c + 1)
                        for i, a in enumerate(h2):
                            mm = pe.matmul(psum[:, q, 0:D], a[:, c, t * P:(t + 1) * P], w2[:, c, :],
                                           start=(c == 0 and i == 0), stop=(c == 7 and i == 1),
                                           skip_group_check=True)
                        if c == 7:
                            mm.then_inc(ff_mm, 1)
                        take(steps, spread(MX_BESIDE[k][8 + t], c, 8))

            def maxima(b):
                for e in range(MXB):
                    g, n = divmod(e, MX_STEPS)
                    j, u = divmod(n, NMX)
                    buf = STACK_OF[g]
                    if n == 0:
                        pe.wait_ge(stacked[buf], stacked_value(b, g))
                    if n == MX_STEPS - 1:
                        pe.wait_ge(m_found, b * 4 + g + 1)
                        turn(psum[:, 4 + e % 2, 0:P], m_col[:, :]).then_inc(mx_mm, 1)
                        yield
                        continue
                    if e == 0:
                        pe.wait_ge(cos_done, b * 4 + 3)
                    elif e >= 2:
                        pe.wait_ge(mx_read, b * MXB + e - 1)
                    for t, a, end, col in MX_UNITS[u]:
                        mm = pe.matmul(psum[:, 4 + e % 2, col:col + end - a],
                                       q_st[0:KR, buf, j, t * P:(t + 1) * P], k_st[0:KR, buf, j, a:end],
                                       start=True, stop=True, skip_group_check=True)
                    mm.then_inc(mx_mm, 1)
                    yield

            def ring_wait(b, f, use):
                i = SLOT[use]
                if i < 2:
                    if f is not None:
                        pe.wait_ge(y_done, f * 8 + 8)
                    else:
                        pe.wait_ge(v_copied, 2)
                else:
                    kind, g, u, h = ST_RING[i - 2]
                    if kind == "st":
                        pe.wait_ge(exp_done, b * 72 + 18 * g + 2 * u + h + 1)
                    else:
                        pe.wait_ge(normed, b * 4 + g + 1)
                return 2 * (i % 2)

            def scores_t(b, f, g, u, h):
                if u == 0 and h == 0:
                    pe.wait_ge(m_rows, b * 192 + 48 * (g + 1))
                q = ring_wait(b, f, ("st", g, u, h))
                for i in range(2):
                    for t, a, e, col in ST_UNITS[u]:
                        mm = pe.matmul(psum[:, q + i, col:col + e - a],
                                       k_st[0:KM, STACK_OF[g], 2 * h + i, t * P:(t + 1) * P],
                                       q_st[0:KM, STACK_OF[g], 2 * h + i, a:e],
                                       start=True, stop=True, skip_group_check=True)
                mm.then_inc(st_mm, 1)

            def times_v(b, g, u):
                if u == 0:
                    if g == 0:
                        pe.wait_ge(cos_done, b * 4 + 4)
                    else:
                        pe.wait_ge(o_copied, b * 4 + g)
                pe.wait_ge(exp_done, b * 72 + 18 * g + 2 * u + 2)
                if u in MASKED:
                    pe.wait_ge(mask_done, b * 4 * NMASK + NMASK * g + MASKED.index(u) + 1)
                for t, a, e, col in ST_UNITS[u]:
                    bank, first = a // BANK, a - a // BANK * BANK
                    for j in range(HG):
                        mm = pe.matmul(psum[32 * j:32 * j + 32, 6 + bank, first:first + e - a],
                                       v_all[:, t, (HG * g + j) * V_ROW:(HG * g + j) * V_ROW + 32],
                                       probs[:, (NU * g + u) % RING, j, col:col + e - a],
                                       start=(t == 0), stop=(u == NU - 1 or (bank == 0 and u == 4)),
                                       skip_group_check=True)
                mm.then_inc(pv_done, 1)

            def turn_o(b, f, g):
                pe.wait_ge(o_copied, b * 4 + g + 1)
                q = ring_wait(b, f, ("ot", g, 0, 0))
                for t in range(T):
                    mm = turn(psum[:, q + t // 4, (t % 4) * P:(t % 4 + 1) * P], o_t[:, t * P:(t + 1) * P])
                mm.then_inc(ot_mm, 1)

            def attention(b, f, steps, last):
                for g in range(G):
                    for u in range(NU):
                        n = MX_AT[NU * g + u]
                        if g == G - 1 and u == 0 and not last:
                            project_qk(b + 1, 0, 0)
                            project_qk(b + 1, 0, 1)
                        scores_t(b, f, g, u, 0)
                        take(steps, spread(n, 0, 3))
                        scores_t(b, f, g, u, 1)
                        take(steps, spread(n, 1, 3))
                        if u == 3 and g > 0:
                            turn_o(b, f, g - 1)
                        if u >= LAG:
                            times_v(b, g, u - LAG)
                        elif g > 0:
                            times_v(b, g - 1, NU - LAG + u)
                        take(steps, spread(n, 2, 3))
                        if g == G - 2 and u >= NU - 2 and not last:
                            turn_x(b + 1, u - NU + 2)
                        if g == G - 1 and u in (4, 5) and not last:
                            project_qk(b + 1, 1, u - 4)
                for u in range(NU - LAG, NU):
                    times_v(b, G - 1, u)

            def out_project(b, f, last):
                if not last:
                    project_v(b + 1, 0)
                turn_o(b, f, G - 1)
                if not last:
                    project_v(b + 1, 1)
                pe.wait_ge(normed, b * 4 + 4)
                for h in range(2):
                    if h == 1 and not last:
                        pe.wait_ge(v_copied, (b + 1) * 2 + 2)
                    elif h == 1:
                        pe.wait_ge(exp_done, b * 72 + 72)
                    for c in range(NC):
                        for t in range(4):
                            mm = turn(psum[:, 2 - 2 * h + c, t * P:(t + 1) * P],
                                      attn[:, 4 * h + t, c * P:(c + 1) * P])
                    mm.then_inc(at_mm, 1)
                if not last:
                    pe.wait_ge(cos_done, (b + 1) * 4 + 2)
                pe.wait_ge(mx_read, b * MXB + MXB)
                pe.wait_ge(o_copied, b * 4 + 4)
                for t in range(T):
                    if t % 4 == 0:
                        pe.wait_ge(at_copied, b * 2 + t // 4 + 1)
                    for c in range(NC):
                        mm = pe.matmul(psum[:, 4 + t // 2, (t % 2) * D:(t % 2 + 1) * D],
                                       attn_t[:, c, t * P:(t + 1) * P], w_o[:, c, :],
                                       start=(c == 0), stop=(c == NC - 1), skip_group_check=True)
                    mm.then_inc(wo_mm, 1)

            def one(b, f, last=False):
                for n in (2, 3):
                    project_qk(b, n, 0)
                    project_qk(b, n, 1)
                steps = maxima(b)
                if f is not None:
                    turn_x1(f)
                    mlp(f, 0, steps)
                    mlp(f, 1, steps)
                else:
                    take(steps, MX_MLP)
                attention(b, f, steps, last)
                out_project(b, f, last)

            pe.wait_ge(consts_in, 16 * 11)
            pe.wait_ge(ready, 1)
            turn_x(0, 0)
            turn_x(0, 1)
            for n in range(2):
                project_qk(0, n, 0)
                project_qk(0, n, 1)
            project_v(0, 0)
            project_v(0, 1)
            one(0, None)
            with pe.Fori(0, B - 2) as i:
                one(i + 1, i)
            one(B - 1, B - 2, last=True)
            turn_x1(B - 1)
            mlp(B - 1, 0)
            mlp(B - 1, 1)

        @block.scalar
        def _(act):
            def copy_xt(b, h):
                act.wait_ge(xt_mm, b * 2 + h + 1)
                act.activation(x_t[:, :, h * BANK:(h + 1) * BANK], psum[:, 4:6, :], ACT.Copy).then_inc(xt_copied, 1)

            def copy_v(b, h):
                act.wait_ge(v_mm, b * 2 + h + 1)
                act.activation(v_ones[:, 4 * h:4 * h + 4, :, 0:HD],
                               psum[:, 0:2, :].rearrange("p b (t h d) -> p (b t) h d", t=2, d=HD),
                               ACT.Copy).then_inc(v_copied, 1)

            def turn_x1(f):
                for h in range(2):
                    act.wait_ge(x1t_mm, f * 2 + h + 1)
                    act.activation(x1_hi[:, :, h * BANK:(h + 1) * BANK], psum[:, 2 * h:2 * h + 2, :], ACT.Copy)\
                        .then_inc(x1_hi_done, 1)

            def mlp(f, k):
                for n in range(16):
                    act.wait_ge(ff_mm, f * 40 + 20 * k + n + 1)
                    h = (h1 if n < 8 else h2)[0]
                    act.activation(h[:, n % 8, :], psum[:, n % 4, :], ACT.Relu).then_inc(h_hi, 1)

            def exps(b, g, u, h):
                act.wait_ge(st_mm, b * 72 + 18 * g + 2 * u + h + 1)
                U = NU * g + u
                if U >= RING and h == 0:
                    act.wait_ge(pv_done, b * 36 + U - RING + 1)
                q = 2 * (SLOT[("st", g, u, h)] % 2)
                act.activation(probs[:, U % RING, 2 * h:2 * h + 2, :], psum[:, q:q + 2, :], ACT.Exp,
                               scale=SCALE).then_inc(exp_done, 1)

            def copy_o(b, g):
                act.wait_ge(pv_done, b * 36 + NU * (g + 1))
                if g > 0:
                    act.wait_ge(ot_mm, b * 4 + g)
                act.activation(o_t[:, :], psum[:, 6:8, :], ACT.Copy).then_inc(o_copied, 1)

            def attention(b, last):
                for g in range(G):
                    for u in range(NU):
                        if u == LAG and g > 0:
                            copy_o(b, g - 1)
                        exps(b, g, u, 0)
                        exps(b, g, u, 1)
                        if g == G - 2 and u >= NU - 2 and not last:
                            copy_xt(b + 1, u - NU + 2)
                copy_o(b, G - 1)
                if not last:
                    copy_v(b + 1, 0)
                    copy_v(b + 1, 1)
                for h in range(2):
                    act.wait_ge(at_mm, b * 2 + h + 1)
                    act.activation(attn_t[:, :, h * BANK:(h + 1) * BANK], psum[:, 2 - 2 * h:4 - 2 * h, :], ACT.Copy)\
                        .then_inc(at_copied, 1)

            def one(b, f, last=False):
                if f is not None:
                    turn_x1(f)
                    mlp(f, 0)
                    mlp(f, 1)
                attention(b, last)

            act.wait_ge(pool_ready, 1)
            act.wait_ge(ready, 2)
            for h in range(2):
                copy_xt(0, h)
            for h in range(2):
                copy_v(0, h)
            one(0, None)
            with act.Fori(0, B - 2) as i:
                one(i + 1, i)
            one(B - 1, B - 2, last=True)
            turn_x1(B - 1)
            mlp(B - 1, 0)
            mlp(B - 1, 1)

        @block.gpsimd
        def _(pool):
            pool.memset(v_all[:, :, :], 1.0).then_inc(pool_ready, 1)

            def keep_x(b):
                pool.wait_ge(x_loaded, b * 16 + 16)
                if not first(b):
                    pool.wait_ge(res_done, b * T)
                pool.sem_inc(pool_passed, 1)
                pool.tensor_copy(x_res[:, :, :], x_in[:, :, :]).then_inc(x_kept, 1)

            def times_sin(b, n):
                pool.wait_ge(swap_done, b * 4 + n + 1)
                if n or not first(b):
                    pool.wait_ge(parts_done, b * 4 + n)
                pool.tensor_tensor(rest, swapped, sin_sb[:, :], ALU.mult).then_inc(sin_done, 1)

            def inv_std(done, eps_ready, n, dst, src, width):
                pool.wait_ge(eps_ready, n)
                pool.tensor_tensor(dst, src, minus_half[:, 0:width], ALU.pow).then_inc(done, 1)

            def masks(b, g, which=MASKED):
                for u in which:
                    pool.wait_ge(exp_done, b * 72 + 18 * g + 2 * u + 2)
                    pool.sem_inc(pool_passed, 1)
                    for col in DIAG[u]:
                        blk = probs[:, (NU * g + u) % RING, :, col:col + P]
                        op = pool.affine_select(out=blk, in_=blk, compare_op=ALU.is_ge, fill=0.0, base=0,
                                                pattern=[[0, HG], [1, P]], channel_multiplier=-1)
                    op.then_inc(mask_done, 1)

            def one(b, f, last=False):
                keep_x(b)
                times_sin(b, 2)
                times_sin(b, 3)
                if f is not None:
                    inv_std(rstd2_done, eps2_done, f * 2 + 1, rstd2[:, :], var_eps2[:, :], 4)
                    inv_std(rstd2_done, eps2_done, f * 2 + 2, rstd2[:, :], var_eps2[:, :], 4)
                for g in range(G - 1):
                    masks(b, g)
                masks(b, G - 1, MASKED[:1])
                if not last:
                    times_sin(b + 1, 0)
                masks(b, G - 1, MASKED[1:])
                if not last:
                    times_sin(b + 1, 1)
                for h in range(2):
                    inv_std(rstd_done, eps_done, b * 2 + h + 1, rstd[:, 4 * h:4 * h + 4], var_eps[:, 4 * h:4 * h + 4], 4)

            pool.wait_ge(ready, 1)
            pool.wait_ge(consts_in, 16 * 11)
            times_sin(0, 0)
            times_sin(0, 1)
            one(0, None)
            with pool.Fori(0, B - 2) as i:
                one(i + 1, i)
            one(B - 1, B - 2, last=True)
            inv_std(rstd2_done, eps2_done, (B - 1) * 2 + 1, rstd2[:, :], var_eps2[:, :], 4)
            inv_std(rstd2_done, eps2_done, (B - 1) * 2 + 2, rstd2[:, :], var_eps2[:, :], 4)

        @block.vector
        def _(dve):
            dumps = [0]
            SWAP = [i ^ 1 for i in range(32)]

            def rope(b, n):
                bank = 6 if n == 3 else 4
                ps = psum[:, bank:bank + 2, :].rearrange("p b n -> p (b n)")
                dve.wait_ge(qk_mm, b * 4 + n + 1)
                dve.sem_inc(dve_passed, 1)
                dve.stream_shuffle(swapped, ps, SWAP).then_inc(swap_done, 1)
                yield
                if n or not first(b):
                    dve.wait_ge(parts_done, b * 4 + n)
                dve.tensor_tensor(turned, ps, cos_sb[:, :], ALU.mult).then_inc(cos_done, 1)
                yield
                dve.wait_ge(cos_done, b * 4 + n + 1)
                dve.wait_ge(sin_done, b * 4 + n + 1)
                dve.tensor_tensor(turned, turned, rest, ALU.add).then_inc(turned_done, 1)
                yield
                if n >= 2 or not first(b):
                    dve.wait_ge(stored[n % 2], b * 32 + (n // 2) * 16)
                dve.wait_ge(turned_done, b * 4 + n + 1)
                dve.tensor_copy(parts[:, n % 2, 0, :], turned).then_inc(hi_done, 1)
                yield
                dve.wait_ge(hi_done, b * 4 + n + 1)
                dve.tensor_tensor(rest, turned, parts[:, n % 2, 0, :], ALU.subtract).then_inc(rest_done, 1)
                yield
                dve.wait_ge(rest_done, b * 4 + n + 1)
                dve.tensor_copy(parts[:, n % 2, 1, :], rest).then_inc(mid_done, 1)
                yield
                dve.wait_ge(mid_done, b * 4 + n + 1)
                dve.tensor_tensor(parts[:, n % 2, 2, :], rest, parts[:, n % 2, 1, :], ALU.subtract)\
                    .then_inc(parts_done, 1)
                yield

            def turn_x1(f):
                for h in range(2):
                    dve.wait_ge(x1_hi_done, f * 2 + h + 1)
                    dve.tensor_tensor(x1_lo[:, :, h * BANK:(h + 1) * BANK], psum[:, 2 * h:2 * h + 2, :],
                                      x1_hi[:, :, h * BANK:(h + 1) * BANK], ALU.subtract).then_inc(x1_lo_done, 1)

            def mlp(f, k, late=None, steps=None):
                def lo(n):
                    h = h1 if n < 8 else h2
                    dve.wait_ge(h_hi, f * 32 + 16 * k + n + 1)
                    dve.scalar_tensor_tensor(out=h[1][:, n % 8, :], in0=psum[:, n % 4, :], scalar=0.0,
                                             in1=h[0][:, n % 8, :], op0=ALU.max, op1=ALU.subtract)\
                        .then_inc(h_lo, 1)

                for n in range(8):
                    lo(n)
                    if n == 3 and k == 1:
                        finish(f, 0)
                for n in range(8):
                    if n:
                        lo(7 + n)
                    if k == 0:
                        take(late, ROPE_BESIDE[n])
                    take(steps, MX_BESIDE[k][n])
                lo(15)
                if k == 0:
                    dve.wait_ge(out_stored, f * 32 + 16)
                else:
                    dve.wait_ge(out_stored, f * 32 + 32)
                for t in range(4):
                    take(steps, MX_BESIDE[k][8 + t])
                    dve.wait_ge(ff_mm, f * 40 + 20 * k + 17 + t)
                    dve.scalar_tensor_tensor(out=y[:, t, :], in0=psum[:, t, 0:D], scalar=factor[:, 0:1],
                                             in1=x1[:, 4 * k + t, :], op0=ALU.mult, op1=ALU.add)\
                        .then_inc(y_done, 1)
                for t in range(4):
                    dve.wait_ge(y_done, f * 8 + 4 * k + t + 1)
                    dve.bn_stats(stats2[:, t, :], y[:, t, :]).then_inc(stat2_done, 1)
                for t in range(4):
                    dve.wait_ge(stat2_done, f * 8 + 4 * k + t + 1)
                    dve.sem_inc(dve_passed, 1)
                    dve.bn_aggr(mean_var2[:, t, :], stats2[:, t, :]).then_inc(aggr2_done, 1)
                dve.wait_ge(aggr2_done, f * 8 + 4 * k + 4)
                dve.tensor_scalar(var_eps2[:, :], mean_var2[:, :, 1], EPS, None, ALU.add).then_inc(eps2_done, 1)

            def finish(f, k):
                dve.wait_ge(rstd2_done, f * 2 + k + 1)
                for t in range(4):
                    dve.tensor_scalar(y[:, t, :], y[:, t, :], mean_var2[:, t, 0:1], rstd2[:, t:t + 1],
                                      ALU.subtract, ALU.mult).then_inc(out_done, 1)

            def maxima(b):
                for e in range(MXB):
                    g, n = divmod(e, MX_STEPS)
                    j, u = divmod(n, NMX)
                    if n == MX_STEPS - 1:
                        split_maxima(b, g, e)
                        yield
                        continue
                    if n == 0 and (g >= 2 or not first(b)):
                        dve.wait_ge(m_found, b * 4 + g - 1)
                    dve.wait_ge(mx_mm, b * MXB + e + 1)
                    bank = 4 + e % 2
                    for t, a, end, col in MX_UNITS[u]:
                        diag = end == (t + 1) * P
                        wide = end - a - (P if diag else 0)
                        if wide:
                            op = dve.tensor_reduce(mx[:, g % 2, j, t, a // BANK:a // BANK + 1],
                                                   psum[:, bank, col:col + wide], AX.X, ALU.max)
                        if diag:
                            dumps[0] += 1
                            op = dve.tensor_tensor_reduce(dump[:, dumps[0] % 4, :],
                                                          psum[:, bank, col + wide:col + wide + P],
                                                          tri_sb[:, :], 1.0, LOWEST, ALU.add, ALU.max,
                                                          mx[:, g % 2, j, t, 2:3])
                    op.then_inc(mx_read, 1)
                    if n == MX_STEPS - 2:
                        dve.wait_ge(mx_read, b * MXB + e + 1)
                        if g or not first(b):
                            dve.wait_ge(mx_mm, b * MXB + g * MX_STEPS)
                        dve.tensor_reduce(m_col[:, 0:HG * T], mx[:, g % 2].rearrange("p j t a -> p (j t) a"), AX.X,
                                          ALU.max).then_inc(m_found, 1)
                    yield

            def split_maxima(b, g, e):
                mt = psum[0:HG * T, 4 + e % 2, 0:P]
                dve.wait_ge(mx_mm, b * MXB + e + 1)
                dve.wait_ge(m_rows, b * 192 + 48 * g)
                dve.tensor_scalar(m_parts[:, 0, :], mt, -1.0, None, ALU.mult).then_inc(m_hi, 1)
                dve.wait_ge(m_hi, b * 4 + g + 1)
                dve.scalar_tensor_tensor(out=m_rest[:, :], in0=mt, scalar=-1.0, in1=m_parts[:, 0, :],
                                         op0=ALU.mult, op1=ALU.subtract).then_inc(mx_read, 1)
                dve.wait_ge(mx_read, b * MXB + e + 1)
                dve.tensor_copy(m_parts[:, 1, :], m_rest[:, :]).then_inc(m_mid, 1)
                dve.wait_ge(m_mid, b * 4 + g + 1)
                dve.tensor_tensor(m_parts[:, 2, :], m_rest[:, :], m_parts[:, 1, :], ALU.subtract)\
                    .then_inc(m_split, 1)

            def normalise(b, g):
                q = 2 * (SLOT[("ot", g, 0, 0)] % 2)
                o = psum[:, q:q + 2, :].rearrange("p b (t j d) -> p (b t) j d", t=4, j=HG)
                dve.wait_ge(ot_mm, b * 4 + g + 1)
                if g or not first(b):
                    dve.wait_ge(normed, b * 4 + g)
                dve.reciprocal(recip[:, :, :], o[:, :, :, HD]).then_inc(recip_done, 1)
                dve.wait_ge(recip_done, b * 4 + g + 1)
                if g == 0 and not first(b):
                    dve.wait_ge(at_mm, b * 2)
                dst = attn[:, :, HG * HD * g:HG * HD * (g + 1)].rearrange("p t (j d) -> p t j d", j=HG)
                dve.tensor_tensor(dst, o[:, :, :, 0:HD],
                                  recip[:, :, :].unsqueeze(3).to_broadcast([P, T, HG, HD]), ALU.mult)\
                    .then_inc(normed, 1)

            def attention(b, f, steps, last):
                for g in range(G - 1):
                    for u in range(NU):
                        take(steps, MX_AT[NU * g + u])
                        if g == 0 and u == 0 and f is not None:
                            finish(f, 1)
                        if u == 3 and g > 0:
                            normalise(b, g - 1)
                ahead = None if last else rope(b + 1, 0)
                take(ahead, 5)
                normalise(b, G - 2)
                if not last:
                    run(ahead)
                    run(rope(b + 1, 1))
                normalise(b, G - 1)

            def norm1(b):
                for h in range(2):
                    tiles = range(4 * h, 4 * h + 4)
                    for t in tiles:
                        dve.wait_ge(wo_mm, b * T + t // 2 * 2 + 2)
                        if t == 0:
                            dve.wait_ge(x_kept, b + 1)
                            if not first(b):
                                dve.wait_ge(y_done, b * 8)
                                dve.wait_ge(x1t_mm, b * 2)
                        dve.tensor_tensor(x1[:, t, :], psum[:, 4 + t // 2, (t % 2) * D:(t % 2 + 1) * D],
                                          x_res[:, t, :], ALU.add).then_inc(res_done, 1)
                    for t in tiles:
                        dve.wait_ge(res_done, b * T + t + 1)
                        dve.bn_stats(stats[:, t, :], x1[:, t, :]).then_inc(stat_done, 1)
                    for t in tiles:
                        dve.wait_ge(stat_done, b * T + t + 1)
                        dve.sem_inc(dve_passed, 1)
                        dve.bn_aggr(mean_var[:, t, :], stats[:, t, :]).then_inc(aggr_done, 1)
                    dve.wait_ge(aggr_done, b * T + 4 * h + 4)
                    dve.tensor_scalar(var_eps[:, 4 * h:4 * h + 4], mean_var[:, 4 * h:4 * h + 4, 1], EPS, None,
                                      ALU.add).then_inc(eps_done, 1)
                for h in range(2):
                    dve.wait_ge(rstd_done, b * 2 + h + 1)
                    for t in range(4 * h, 4 * h + 4):
                        dve.tensor_scalar(x1[:, t, :], x1[:, t, :], mean_var[:, t, 0:1], rstd[:, t:t + 1],
                                          ALU.subtract, ALU.mult).then_inc(x1_done, 1)

            def run(gen):
                for _ in gen:
                    pass

            def chain(*gens):
                for gen in gens:
                    yield from gen

            def one(b, f, last=False):
                late, steps = chain(rope(b, 2), rope(b, 3)), maxima(b)
                if f is not None:
                    turn_x1(f)
                    mlp(f, 0, late, steps)
                    mlp(f, 1, None, steps)
                else:
                    run(late)
                    take(steps, MX_MLP)
                attention(b, f, steps, last)
                norm1(b)

            dve.memset(m_col[:, :], 0.0)
            dve.memset(k_st[96:128, :, :, :], 1.0)
            dve.memset(minus_half[:, :], -0.5)
            dve.memset(mx[:, :, :, :, :], LOWEST).then_inc(ready, 1)
            dve.wait_ge(w_in, 16 * 6)
            step = sem("setup_step")
            dve.tensor_scalar(s_sign[:, :], s_in[:, :], 0.0, 2.0, ALU.is_ge, ALU.mult).then_inc(step, 1)
            dve.wait_ge(step, 1)
            dve.tensor_scalar(s_sign[:, :], s_sign[:, :], -1.0, None, ALU.add).then_inc(step, 1)
            dve.wait_ge(step, 2)
            dve.tensor_tensor(s_abs[:, :], s_in[:, :], s_sign[:, :], ALU.mult).then_inc(step, 1)
            dve.wait_ge(step, 3)
            dve.tensor_tensor(s_prod[:, :], s_abs[:, 0:1], s_abs[:, 1:2], ALU.mult).then_inc(step, 1)
            dve.wait_ge(step, 4)
            dve.scalar_tensor_tensor(out=factor[:, :], in0=s_prod[:, :], scalar=OUT_FACTOR, in1=s_in[:, 2:3],
                                     op0=ALU.mult, op1=ALU.mult).then_inc(step, 1)
            dve.tensor_tensor(w0[:, :, :], k0_u8[:, 0:2, :], k0_u8[:, 2:4, :], ALU.subtract).then_inc(step, 1)
            dve.tensor_scalar(w1[:, :, :], k1_u8, 2.0 * W1_SCALE, -W1_SCALE, ALU.mult, ALU.add).then_inc(step, 1)
            dve.tensor_scalar(w2[:, :, :], k2_u8, 2.0, -1.0, ALU.mult, ALU.add).then_inc(step, 1)
            dve.wait_ge(step, 8)
            dve.tensor_scalar(w0[:, :, :], w0[:, :, :], s_sign[:, 0:1], None, ALU.mult).then_inc(step, 1)
            dve.tensor_scalar(w1[:, :, :], w1[:, :, :], s_sign[:, 1:2], None, ALU.mult).then_inc(ready, 1)
            dve.wait_ge(pool_ready, 1)
            dve.wait_ge(consts_in, 16 * 11)

            run(rope(0, 0))
            run(rope(0, 1))
            one(0, None)
            with dve.Fori(0, B - 2) as i:
                one(i + 1, i)
            one(B - 1, B - 2, last=True)
            turn_x1(B - 1)
            mlp(B - 1, 0)
            mlp(B - 1, 1)
            finish(B - 1, 1)


NAMES = ("x", "wq", "wk", "wv", "wo", "k0", "k1", "k2", "s0", "s1", "s2")


def rope_tables():
    inv = (np.float32(1.0) / np.float32(10000.0) ** (np.arange(0, HD, 2, dtype=np.float32) / np.float32(HD)))
    ang = (np.arange(S, dtype=np.float32)[None, :] * inv.astype(np.float32)[:, None]).astype(np.float32)
    row = np.arange(P) % HD
    a = ang[row // 2]
    sign = np.where(row % 2 == 0, -1.0, 1.0)[:, None]
    return np.cos(a.astype(np.float64)).astype(np.float32), (np.sin(a.astype(np.float64)) * sign).astype(np.float32)


def kernel(L0_attn_x, L0_attn_wq, L0_attn_wk, L0_attn_wv, L0_attn_wo, L0_ffn_k0, L0_ffn_k1, L0_ffn_k2,
           L0_ffn_s0, L0_ffn_s1, L0_ffn_s2):
    import concourse.bacc as bacc
    from concourse.bass_utils import run_bass_kernel_spmd

    cos, sin = rope_tables()
    row, col = np.arange(P)[:, None], np.arange(P)[None, :]
    arrays = {
        "x": np.ascontiguousarray(L0_attn_x),
        "wq": np.ascontiguousarray(L0_attn_wq),
        "wk": np.ascontiguousarray(L0_attn_wk),
        "wv": np.ascontiguousarray(L0_attn_wv),
        "wo": np.ascontiguousarray(L0_attn_wo),
        "k0": np.ascontiguousarray(L0_ffn_k0),
        "k1": np.ascontiguousarray(L0_ffn_k1),
        "k2": np.ascontiguousarray(L0_ffn_k2),
        "s0": np.asarray(L0_ffn_s0).reshape(1),
        "s1": np.asarray(L0_ffn_s1).reshape(1),
        "s2": np.asarray(L0_ffn_s2).reshape(1),
        "cos": cos,
        "sin": sin,
        "ident": np.eye(P, dtype=np.float32),
        "tri": np.where(col <= row, 0.0, -1.0e38).astype(np.float32),
    }
    nc = bacc.Bacc("TRN2", target_bir_lowering=False, num_devices=1)
    ins = [nc.dram_tensor(f"in_{n}", a.shape, mybir.dt.from_np(a.dtype), kind="ExternalInput").ap()
           for n, a in arrays.items()]
    out = nc.dram_tensor("out", (B, S, D), F32, kind="ExternalOutput").ap()
    scratch = nc.dram_tensor("scratch", (2, 2, 3, P, S), BF16).ap()
    build(nc, *ins, out, scratch)
    r = run_bass_kernel_spmd(nc, [{f"in_{n}": a for n, a in arrays.items()}], core_ids=[0])
    return r.results[0]["out"]
```

```python
from contextlib import ExitStack

import concourse.bass as bass
from concourse import mybir
import numpy as np

F32, BF16, F16, U8 = mybir.dt.float32, mybir.dt.bfloat16, mybir.dt.float16, mybir.dt.uint8
ALU, ACT, AX = mybir.AluOpType, mybir.ActivationFunctionType, mybir.AxisListType

P = 128
B, S, D = 8, 1024, 256
H, HD = 16, 16
T = S // P
F = 1024
HG = 4
G = H // HG
NC = D // P
BANK = 512
EPS = 1e-5
LOWEST = -3.0e38
SCALE = float(HD) ** -0.5
Q_PARTS = (0, 1, 2, 0, 1, 0)
K_PARTS = (0, 0, 0, 1, 1, 2)
KR = HD * len(Q_PARTS)
KM = KR + 3
W1_SCALE = 1.0 / 16
OUT_FACTOR = 2.0 * 2.0 * 2.0 / W1_SCALE

def spread(n, i, of):
    return n * (i + 1) // of - n * i // of


ST_UNITS = (
    ((0, 0, 512, 0),),
    ((0, 512, 1024, 0),),
    ((1, 128, 512, 0), (7, 896, 1024, 384)),
    ((2, 256, 512, 0), (6, 768, 1024, 256)),
    ((3, 384, 512, 0), (5, 640, 1024, 128)),
    ((4, 512, 1024, 0),),
    ((1, 512, 1024, 0),),
    ((2, 512, 1024, 0),),
    ((3, 512, 1024, 0),),
)
NU = len(ST_UNITS)
DIAG = tuple(tuple(c for k, a, b, c in u if a == k * P) for u in ST_UNITS)
MASKED = tuple(u for u in range(NU) if DIAG[u])
MX_UNITS = (
    ((7, 0, 512, 0),),
    ((7, 512, 1024, 0),),
    ((6, 0, 512, 0),),
    ((6, 512, 896, 0), (0, 0, 128, 384)),
    ((5, 0, 512, 0),),
    ((5, 512, 768, 0), (1, 0, 256, 256)),
    ((4, 0, 512, 0),),
    ((3, 0, 512, 0),),
    ((2, 0, 384, 0), (4, 512, 640, 384)),
)
NMX = len(MX_UNITS)
TURN_LATER = 2
MX_ORDER = []
for g in range(G):
    for n in range(HG * NMX):
        MX_ORDER.append((g, n // NMX, n % NMX))
        if g > 0 and n == TURN_LATER - 1:
            MX_ORDER.append((g - 1, None, None))
MX_ORDER.append((G - 1, None, None))
MXB = len(MX_ORDER)
TURN_AT = [MX_ORDER.index((g, None, None)) for g in range(G)]
ROPE_BESIDE = (2, 1, 0, 2, 1, 0, 0, 0)
ROUND_AT = {10: (2, 0), 11: (2, 1), 14: (3, 0), 15: (3, 1)}
MX_BESIDE = ((0, 4, 5, 3, 4, 5, 5, 5, 2, 2, 2, 1), (4, 5, 5, 4, 5, 5, 5, 4, 2, 2, 1, 1))
MX_MLP = sum(map(sum, MX_BESIDE))
MX_FIRST = TURN_AT[0] + 6
OT_UNIT, XT_UNIT = 3, 6


def shares(total, weights):
    sums = [sum(weights[:i]) for i in range(len(weights) + 1)]
    return tuple(total * b // sums[-1] - total * a // sums[-1] for a, b in zip(sums, sums[1:]))


MX_AT = (shares(TURN_AT[2] - TURN_LATER + 1 - MX_MLP, (0, 0, 3, 2, 3, 2, 2, 3, 3, 3, 3, 3))
         + shares(MXB - 2 - TURN_AT[2] + TURN_LATER, (0, 2, 4, 0, 4, 4, 4, 4, 4, 0, 4, 4, 0)) + (0,) * (2 + NU))
MX_AT_FIRST = (shares(TURN_AT[1] + 1 - MX_FIRST, (4, 4, 4, 4, 4, 4, 4))
               + shares(MXB - 1 - TURN_AT[1] - 1, (4, 4) + (4, 4, 4, 0, 4, 4, 0, 4, 4) + (4, 4, 4, 0, 4, 4, 0))
               + (0,) * (2 + NU))
NORM_BESIDE = (2, 2, 1, 2, 2, 0, 0, 0)
NORM_AT = (0, 2, 1, 1, 1, 2, 2)
MX_ROPE_FIRST = (0, 2, 4, 0, 6, 0)
assert len(MX_AT) == len(MX_AT_FIRST) == G * NU
STACK_OF = (0, 1, 2, 0)
V_ROW = HD + 1
LAG = 2
RING = 3


def take(steps, n):
    if steps is not None:
        for _ in range(n):
            next(steps, None)


def first(b):
    return isinstance(b, int) and b == 0


def build(nc, x, wq, wk, wv, wo, k0, k1, k2, s0, s1, s2, cos, sin, ident, tri, out, scratch):
    with ExitStack() as ctx:
        def sb(name, shape, dt):
            return ctx.enter_context(nc.sbuf_tensor(name, shape, dt))

        def sem(name):
            return ctx.enter_context(nc.semaphore(name))

        psum = ctx.enter_context(nc.psum_tensor("psum", [P, 8, BANK], F32))

        w_qkv = sb("w_qkv", [P, NC, 3, D], F32)
        w_o = sb("w_o", [P, NC, D], F32)
        w0 = sb("w0", [P, NC, F], F16)
        w1 = sb("w1", [P, F // P, F], F16)
        w2 = sb("w2", [P, F // P, D], F16)
        cos_sb = sb("cos_sb", [P, S], F32)
        sin_sb = sb("sin_sb", [P, S], F32)
        id_sb = sb("id_sb", [P, P], F32)
        tri_sb = sb("tri_sb", [P, P], F32)
        id_bf = sb("id_bf", [P, P], BF16)
        tri_bf = sb("tri_bf", [P, P], BF16)
        s_in = sb("s_in", [P, 3], F32)
        s_sign = sb("s_sign", [P, 3], F32)
        s_abs = sb("s_abs", [P, 3], F32)
        s_prod = sb("s_prod", [P, 1], F32)
        factor = sb("factor", [P, 1], F32)
        minus_half = sb("minus_half", [P, T], F32)
        minus_one = sb("minus_one", [P, 1], F32)
        w1_scale = sb("w1_scale", [P, 1], F32)
        w1_bias = sb("w1_bias", [P, 1], F32)
        x_in = sb("x_in", [P, T, D], F32)
        x_res = sb("x_res", [P, T, D], F32)
        x1 = sb("x1", [P, T, D], F32)
        v_all = sb("v_all", [P, T, H * V_ROW + 32 - V_ROW], F32)
        v_ones = v_all[:, :, 0:H * V_ROW].rearrange("p t (h d) -> p t h d", d=V_ROW)
        parts = sb("parts", [P, 2, 3, S], BF16)
        q_st = sb("q_st", [P, 3, HG, S], BF16)
        k_st = sb("k_st", [P, 3, HG, S], BF16)
        rope_buf = sb("rope_buf", [P, 3, S], F32)
        swapped, turned, rest = rope_buf[:, 0, :], rope_buf[:, 1, :], rope_buf[:, 2, :]
        region = sb("region", [P, 8192], F32)
        probs = region[:, 0:RING * HG * BANK].rearrange("p (r j n) -> p r j n", r=RING, j=HG)
        x_t = region[:, 6144:8192].rearrange("p (c n) -> p c n", c=NC)
        halves = region[:, :].bitcast(F16).rearrange("p (a f n) -> p a f n", a=4, f=F // P)
        h1, h2 = (halves[:, 0], halves[:, 1]), (halves[:, 2], halves[:, 3])
        bits = region[:, :].bitcast(U8)
        k0_u8 = bits[:, 0:4 * F].rearrange("p (c n) -> p c n", c=4)
        k1_u8 = bits[:, 4 * F:12 * F].rearrange("p (c n) -> p c n", c=8)
        w0_diff = bits[:, 14 * F:18 * F].bitcast(F16).rearrange("p (c n) -> p c n", c=NC)
        k2_u8 = bits[:, 12 * F:14 * F].rearrange("p (c n) -> p c n", c=8)
        o_t = sb("o_t", [P, S], F32)
        attn = sb("attn", [P, T, D], F32)
        attn_t = region[:, 0:NC * S].rearrange("p (c n) -> p c n", c=NC)
        x1_hi = sb("x1_hi", [P, NC, S], F16)
        x1_lo = sb("x1_lo", [P, NC, S], F16)
        y = sb("y", [P, 4, D], F32)
        recip = sb("recip", [P, T, HG], F32)
        mx = sb("mx", [P, 2, HG, T, 3], F32)
        m_col = sb("m_col", [P, P], F32)
        m_rest = sb("m_rest", [HG * T, P], F32)
        m_parts = sb("m_parts", [HG * T, 3, P], BF16)
        dump = sb("dump", [P, 4, P], BF16)
        stats = sb("stats", [P, T, 6], F32)
        mean_var = sb("mean_var", [P, T, 2], F32)
        var_eps = sb("var_eps", [P, T], F32)
        rstd = sb("rstd", [P, T], F32)
        stats2 = sb("stats2", [P, 4, 6], F32)
        mean_var2 = sb("mean_var2", [P, 4, 2], F32)
        var_eps2 = sb("var_eps2", [P, 4], F32)
        rstd2 = sb("rstd2", [P, 4], F32)

        id_in, tables_in, w_qkvo_in = sem("id_in"), sem("tables_in"), sem("w_qkvo_in")
        w_in = sem("w_in")
        setup_step, weights_ready = sem("setup_step"), sem("weights_ready")
        x_loaded = sem("x_loaded")
        x_kept = sem("x_kept")
        xt_mm, xt_copied = sem("xt_mm"), sem("xt_copied")
        v_mm, v_copied = sem("v_mm"), sem("v_copied")
        qk_mm = sem("qk_mm")
        swap_done = sem("swap_done")
        cos_done = sem("cos_done")
        sin_done = sem("sin_done")
        turned_done = sem("turned_done")
        hi_done, rest_done, mid_done = sem("hi_done"), sem("rest_done"), sem("mid_done")
        parts_done = sem("parts_done")
        stored = [sem("stored0"), sem("stored1")]
        stacked = [sem("stacked0"), sem("stacked1"), sem("stacked2")]
        mx_mm, mx_read = sem("mx_mm"), sem("mx_read")
        m_found = sem("m_found")
        m_hi, m_mid, m_split = sem("m_hi"), sem("m_mid"), sem("m_split")
        m_rows = sem("m_rows")
        st_mm = sem("st_mm")
        exp_done = sem("exp_done")
        mask_done = sem("mask_done")
        pv_done = sem("pv_done")
        o_copied = sem("o_copied")
        ot_mm = sem("ot_mm")
        recip_done = sem("recip_done")
        normed = sem("normed")
        at_mm, at_copied = sem("at_mm"), sem("at_copied")
        wo_mm = sem("wo_mm")
        res_done, stat_done, aggr_done, eps_done, rstd_done, x1_done = (
            sem("res_done"), sem("stat_done"), sem("aggr_done"), sem("eps_done"), sem("rstd_done"), sem("x1_done"))
        x1t_mm, x1_hi_done, x1_lo_done = sem("x1t_mm"), sem("x1_hi_done"), sem("x1_lo_done")
        ff_mm = sem("ff_mm")
        h_hi, h_lo = sem("h_hi"), sem("h_lo")
        y_done, stat2_done, aggr2_done, eps2_done, rstd2_done, out_done = (
            sem("y_done"), sem("stat2_done"), sem("aggr2_done"), sem("eps2_done"), sem("rstd2_done"), sem("out_done"))
        out_stored = sem("out_stored")
        ready = sem("ready")
        pool_ready = sem("pool_ready")
        mask_ready = sem("mask_ready")

        dve_passed, pool_passed, sp_passed = sem("dve_passed"), sem("pool_passed"), sem("sp_passed")

        NMASK = len(MASKED)

        def mx_bank(b, e):
            return e % 4 if first(b) and e < MX_FIRST else 4 + e % 2

        def stacked_value(b, g):
            return b * 384 + 192 * (1 + (g == 3)) if STACK_OF[g] == 0 else b * 192 + 192

        block = ctx.enter_context(nc.Block())

        @block.sync
        def _(sp):
            sp.sem_inc(out_stored, 16)
            sp.dma_start(id_sb[:, :], ident).then_inc(id_in, 16)
            sp.dma_start(x_in[:, :, :], x[0].rearrange("(t p) d -> p t d", p=P)).then_inc(x_loaded, 16)
            for c in range(NC):
                for n, w in ((1, wq), (2, wk), (0, wv)):
                    sp.dma_start(w_qkv[:, c, n, :], w[c * P:(c + 1) * P, :]).then_inc(w_qkvo_in, 16)
            sp.dma_start(cos_sb[:, :], cos).then_inc(tables_in, 16)
            sp.dma_start(sin_sb[:, :], sin).then_inc(tables_in, 16)
            sp.dma_start(tri_sb[:, :], tri).then_inc(tables_in, 16)
            sp.dma_start(w_o[:, :, :], wo.rearrange("(c p) n -> p c n", p=P)).then_inc(w_qkvo_in, 16)
            for n, s in enumerate((s0, s1, s2)):
                sp.dma_start(s_in[:, n:n + 1], s.partition_broadcast(P)).then_inc(w_in, 16)
            sp.dma_start(k0_u8, k0.rearrange("(c p) n -> p c n", p=P)).then_inc(w_in, 16)
            sp.dma_start(k1_u8, k1.rearrange("(c p) n -> p c n", p=P)).then_inc(w_in, 16)
            sp.dma_start(k2_u8, k2.rearrange("(c p) n -> p c n", p=P)).then_inc(w_in, 16)

            def store_parts(b, n):
                sp.wait_ge(parts_done, b * 4 + n + 1)
                sp.sem_inc(sp_passed, 1)
                sp.dma_start(scratch[n // 2, n % 2].rearrange("r p n -> p r n"), parts[:, n % 2, :, :])\
                    .then_inc(stored[n % 2], 16)

            def stack(b, g):
                c, row, buf = g // 2, (g % 2) * HG * HD, STACK_OF[g]
                if g == 3:
                    sp.wait_ge(st_mm, b * 72 + 18)
                    sp.sem_inc(sp_passed, 1)
                elif not first(b):
                    sp.wait_ge(st_mm, b * 72)
                    sp.sem_inc(sp_passed, 1)
                for qk, st, parts_of in ((0, q_st, Q_PARTS), (1, k_st, K_PARTS)):
                    if row == 0:
                        sp.wait_ge(stored[qk], b * 32 + 16 * c + 16)
                        sp.sem_inc(sp_passed, 1)
                    for r in range(len(Q_PARTS)):
                        src = scratch[c, qk, parts_of[r], row:row + HG * HD, :].rearrange("(j d) n -> d j n", d=HD)
                        sp.dma_start(st[r * HD:(r + 1) * HD, buf, :, :], src).then_inc(stacked[buf], 16)

            def max_rows(b, g):
                sp.wait_ge(m_split, b * 4 + g + 1)
                sp.sem_inc(sp_passed, 1)
                for r in range(3):
                    sp.dma_start(q_st[KR + r:KR + r + 1, STACK_OF[g], :, :].rearrange("p j (t n) -> p (j t) n", n=P),
                                 m_parts[:, r, :]).then_inc(m_rows, 16)

            def load_x(nxt):
                sp.wait_ge(x_kept, nxt)
                sp.sem_inc(sp_passed, 1)
                sp.wait_ge(xt_mm, nxt * 2)
                sp.sem_inc(sp_passed, 1)
                sp.dma_start(x_in[:, :, :], x[nxt].rearrange("(t p) d -> p t d", p=P)).then_inc(x_loaded, 16)

            def store_out(f, c):
                sp.wait_ge(out_done, f * 8 + 4 * (c + 1))
                sp.sem_inc(sp_passed, 1)
                sp.dma_start(out[f, c * BANK:(c + 1) * BANK, :].rearrange("(t p) d -> p t d", p=P), y[:, :, :])\
                    .then_inc(out_stored, 16)

            def one(b, f, last=False):
                stack(b, 0)
                stack(b, 1)
                store_parts(b, 2)
                store_parts(b, 3)
                stack(b, 2)
                if not last:
                    load_x(b + 1)
                max_rows(b, 0)
                if f is not None:
                    store_out(f, 0)
                max_rows(b, 1)
                if f is not None:
                    store_out(f, 1)
                stack(b, 3)
                max_rows(b, 2)
                max_rows(b, 3)
                if not last:
                    store_parts(b + 1, 0)
                    store_parts(b + 1, 1)

            store_parts(0, 0)
            store_parts(0, 1)
            one(0, None)
            with sp.Fori(0, B - 2) as i:
                one(i + 1, i)
            one(B - 1, B - 2, last=True)
            store_out(B - 1, 0)
            store_out(B - 1, 1)
            sp.wait_ge(out_stored, B * 32 + 16)

        @block.tensor
        def _(pe):
            def turn(dst, src):
                return pe.matmul(dst, src, id_sb[:, :], start=True, stop=True, is_transpose=True,
                                 skip_group_check=True)

            def turn_x(b, h):
                if h == 0:
                    pe.wait_ge(x_loaded, b * 16 + 16)
                elif first(b):
                    pe.wait_ge(xt_copied, 1)
                for c in range(NC):
                    for t in range(4):
                        mm = turn(psum[:, 4 + c, t * P:(t + 1) * P], x_in[:, 4 * h + t, c * P:(c + 1) * P])
                mm.then_inc(xt_mm, 1)

            def project_v(b, h):
                if h:
                    pe.wait_ge(v_copied, b * 2 + 1)
                elif first(b):
                    pe.wait_ge(xt_copied, 2)
                else:
                    pe.wait_ge(exp_done, b * 72 - 1)
                for t in range(4 * h, 4 * h + 4):
                    for c in range(NC):
                        mm = pe.matmul(psum[:, t // 2 - 2 * h, (t % 2) * D:(t % 2 + 1) * D],
                                       x_t[:, c, t * P:(t + 1) * P], w_qkv[:, c, 0, :],
                                       start=(c == 0), stop=(c == NC - 1), skip_group_check=True)
                mm.then_inc(v_mm, 1)

            def project_qk(b, n, h):
                bank = 6 if n == 3 else 4
                if h == 0:
                    if n == 0:
                        pe.wait_ge(xt_copied, b * 2 + 2)
                        if not first(b):
                            pe.wait_ge(mx_read, b * MXB)
                    elif n == 1:
                        pe.wait_ge(cos_done, b * 4 + 1)
                        if not first(b):
                            pe.wait_ge(normed, b * 4 - 1)
                    elif first(b):
                        pe.wait_ge(cos_done, 2)
                    else:
                        pe.wait_ge(res_done, b * T - (4 if n == 2 else 0))
                for c in range(NC):
                    mm = pe.matmul(psum[:, bank + h, :],
                                   w_qkv[:, c, 1 + n % 2, (n // 2) * P:(n // 2 + 1) * P],
                                   x_t[:, c, h * BANK:(h + 1) * BANK],
                                   start=(c == 0), stop=(c == NC - 1), skip_group_check=True)
                if h:
                    mm.then_inc(qk_mm, 1)

            def turn_x1(f, h):
                if h == 0:
                    pe.wait_ge(at_copied, f * 2 + 2)
                pe.wait_ge(x1_done, f * T + 4 * h + 4)
                for c in range(NC):
                    for t in range(4):
                        mm = turn(psum[:, 2 * h + c, t * P:(t + 1) * P], x1[:, 4 * h + t, c * P:(c + 1) * P])
                mm.then_inc(x1t_mm, 1)

            def mlp(f, k, b=None, steps=None):
                n = 0

                def bank():
                    nonlocal n
                    if n < 4 and k == 0:
                        pe.wait_ge(x1_lo_done, f * 2 + 1 + n // 2)
                    else:
                        pe.wait_ge(h_lo, f * 32 + 16 * k + n - 3)
                    n += 1
                    return (n - 1) % 4

                for o in range(F // P):
                    q = bank()
                    for c in range(NC):
                        for a in (x1_hi, x1_lo):
                            mm = pe.matmul(psum[:, q, :], w0[:, c, o * P:(o + 1) * P],
                                           a[:, c, k * BANK:(k + 1) * BANK],
                                           start=(c == 0 and a is x1_hi), stop=(c == NC - 1 and a is x1_lo),
                                           skip_group_check=True)
                    mm.then_inc(ff_mm, 1)
                for o in range(F // P):
                    q = bank()
                    for c in range(F // P):
                        if o == 0:
                            pe.wait_ge(h_lo, f * 32 + 16 * k + c + 1)
                        for i, a in enumerate(h1):
                            mm = pe.matmul(psum[:, q, :], w1[:, c, o * P:(o + 1) * P], a[:, c, :],
                                           start=(c == 0 and i == 0), stop=(c == 7 and i == 1),
                                           skip_group_check=True)
                        if c == 7:
                            mm.then_inc(ff_mm, 1)
                        take(steps, spread(MX_BESIDE[k][o], c, 8))
                for t in range(4):
                    q = 6 + t % 2
                    if t >= 2 or k == 1:
                        pe.wait_ge(y_done, f * 8 + 4 * k + t - 1)
                    elif b is not None and t == 0:
                        pe.wait_ge(cos_done, b * 4 + 4)
                    for c in range(F // P):
                        if t == 0:
                            pe.wait_ge(h_lo, f * 32 + 16 * k + 8 + c + 1)
                        for i, a in enumerate(h2):
                            mm = pe.matmul(psum[:, q, 0:D], a[:, c, t * P:(t + 1) * P], w2[:, c, :],
                                           start=(c == 0 and i == 0), stop=(c == 7 and i == 1),
                                           skip_group_check=True)
                        if c == 7:
                            mm.then_inc(ff_mm, 1)
                        take(steps, spread(MX_BESIDE[k][8 + t], c, 8))
                    if k == 1 and b is not None:
                        scores_t(b, f, 0, t // 2, t % 2)

            def maxima(b):
                for e, (g, j, u) in enumerate(MX_ORDER):
                    buf = STACK_OF[g]
                    if j == u == 0:
                        pe.wait_ge(stacked[buf], stacked_value(b, g))
                    if first(b) and e < MX_FIRST:
                        if e >= 4:
                            pe.wait_ge(mx_read, e - 3)
                        elif e == 0:
                            pe.wait_ge(v_copied, 2)
                            pe.wait_ge(mask_ready, 2)
                    elif e == (MX_FIRST if first(b) else 0):
                        pe.wait_ge(cos_done, b * 4 + 3)
                    elif e >= 2:
                        pe.wait_ge(mx_read, b * MXB + e - 1)
                    if j is None:
                        pe.wait_ge(m_found, b * 4 + g + 1)
                        turn(psum[:, mx_bank(b, e), 0:P], m_col[:, :]).then_inc(mx_mm, 1)
                        yield
                        continue
                    for t, a, end, col in MX_UNITS[u]:
                        masked = first(b) and end == (t + 1) * P
                        mm = pe.matmul(psum[:, mx_bank(b, e), col:col + end - a],
                                       q_st[0:KR, buf, j, t * P:(t + 1) * P], k_st[0:KR, buf, j, a:end],
                                       start=True, stop=not masked, skip_group_check=True)
                        if masked:
                            mm = pe.matmul(psum[:, mx_bank(b, e), col + end - a - P:col + end - a], id_bf[:, :],
                                           tri_bf[:, :], start=False, stop=True, skip_group_check=True)
                    mm.then_inc(mx_mm, 1)
                    yield

            def scores_t(b, f, g, u, h):
                if u == 0 and h == 0:
                    pe.wait_ge(m_rows, b * 192 + 48 * (g + 1))
                if g > 0 or u > 0:
                    pe.wait_ge(exp_done, b * 72 + 18 * g + 2 * u + h - 1)
                elif f is not None:
                    pe.wait_ge(h_lo, f * 32 + 30 + 2 * h)
                else:
                    pe.wait_ge(mx_read, MX_FIRST)
                for i in range(2):
                    for t, a, e, col in ST_UNITS[u]:
                        mm = pe.matmul(psum[:, 2 * h + i, col:col + e - a],
                                       k_st[0:KM, STACK_OF[g], 2 * h + i, t * P:(t + 1) * P],
                                       q_st[0:KM, STACK_OF[g], 2 * h + i, a:e],
                                       start=True, stop=True, skip_group_check=True)
                mm.then_inc(st_mm, 1)

            def times_v(b, f, g, u):
                if g == 0 and u == 0 and f is None:
                    pe.wait_ge(cos_done, b * 4 + 4)
                elif g == 0 and u == 0:
                    pe.wait_ge(y_done, f * 8 + 8)
                elif g > 0 and u < 2:
                    pe.wait_ge(o_copied, b * 8 + 2 * g - 1 + u)
                pe.wait_ge(exp_done, b * 72 + 18 * g + 2 * u + 2)
                if u in MASKED:
                    pe.wait_ge(mask_done, b * 4 * NMASK + NMASK * g + MASKED.index(u) + 1)
                pieces = ST_UNITS[u]
                (t, a, e, col) = pieces[0]
                if len(pieces) == 1 and t > 0:
                    pieces = ((t, a, a + BANK // 2, col), (t, a + BANK // 2, e, col + BANK // 2))
                for i, (t, a, e, col) in enumerate(pieces):
                    bank, at = a // BANK, a % BANK
                    for j in range(HG):
                        mm = pe.matmul(psum[32 * j:32 * j + 32, 6 + bank, at:at + e - a],
                                       v_all[:, t, (HG * g + j) * V_ROW:(HG * g + j) * V_ROW + 32],
                                       probs[:, (NU * g + u) % RING, j, col:col + e - a],
                                       start=(t == 0), stop=(u == NU - 1 or (bank == 0 and u == 4)),
                                       skip_group_check=True)
                    if i == 0:
                        yield
                mm.then_inc(pv_done, 1)
                yield

            def turn_o(b, g):
                pe.wait_ge(o_copied, b * 8 + 2 * g + 2)
                q = 4 if g < G - 1 else 2
                for t in range(T):
                    mm = turn(psum[:, q + t // 4, (t % 4) * P:(t % 4 + 1) * P], o_t[:, t * P:(t + 1) * P])
                mm.then_inc(ot_mm, 1)

            def attention(b, f, steps, last):
                taken = MX_MLP if f is not None else MX_FIRST
                for g in range(G):
                    for u in range(NU):
                        n = (MX_AT if f is not None else MX_AT_FIRST)[NU * g + u]
                        ot = u == OT_UNIT and g > 0
                        xt = u == XT_UNIT and g in (1, 2) and not last
                        if g == G - 1 and u == 0 and not last:
                            project_qk(b + 1, 0, 0)
                            project_qk(b + 1, 0, 1)
                        early = f is not None and g == 0 and u < LAG
                        if not early:
                            scores_t(b, f, g, u, 0)
                        after_ot = u == OT_UNIT + 1 and 0 < g < G - 1
                        after_xt = u == XT_UNIT + 1 and g in (1, 2) and not last
                        places = 2 if after_ot or after_xt else 4
                        share = [0] * (4 - places) + [spread(n, i, places) for i in range(places)]
                        take(steps, share[0])
                        if not early:
                            scores_t(b, f, g, u, 1)
                        take(steps, share[1])
                        if u >= LAG:
                            product = times_v(b, f, g, u - LAG)
                        elif g > 0:
                            product = times_v(b, f, g - 1, NU - LAG + u)
                        else:
                            product = None
                        take(product, 1)
                        if ot or xt:
                            assert n == 0
                            pe.wait_ge(mx_read, b * MXB + taken)
                            if g == G - 1 and not last:
                                pe.wait_ge(cos_done, (b + 1) * 4 + 1)
                            if ot:
                                turn_o(b, g - 1)
                            else:
                                turn_x(b + 1, g - 1)
                        if after_ot:
                            pe.wait_ge(normed, b * 4 + g)
                        if after_xt:
                            pe.wait_ge(xt_copied, (b + 1) * 2 + g)
                        take(steps, share[2])
                        take(product, 1)
                        take(steps, share[3])
                        taken += n
                        if g == G - 2 and u == XT_UNIT + 1:
                            take(steps, 1)
                            taken += 1
                        if g == G - 1 and u in (4, 5) and not last:
                            project_qk(b + 1, 1, u - 4)
                assert taken == MXB
                for u in range(NU - LAG, NU):
                    take(times_v(b, f, G - 1, u), 2)

            def out_project(b, f, last):
                if not last:
                    project_v(b + 1, 0)
                pe.wait_ge(exp_done, b * 72 + 72)
                turn_o(b, G - 1)
                if not last:
                    project_v(b + 1, 1)
                pe.wait_ge(normed, b * 4 + 4)
                for h in range(2):
                    if h == 1 and not last:
                        pe.wait_ge(v_copied, (b + 1) * 2 + 2)
                    for c in range(NC):
                        for t in range(4):
                            mm = turn(psum[:, 2 - 2 * h + c, t * P:(t + 1) * P],
                                      attn[:, 4 * h + t, c * P:(c + 1) * P])
                    mm.then_inc(at_mm, 1)
                if not last:
                    pe.wait_ge(cos_done, (b + 1) * 4 + 2)
                pe.wait_ge(mx_read, b * MXB + MXB)
                pe.wait_ge(o_copied, b * 8 + 8)
                for t in range(T):
                    if t % 4 == 0:
                        pe.wait_ge(at_copied, b * 2 + t // 4 + 1)
                    for c in range(NC):
                        mm = pe.matmul(psum[:, 4 + t // 2, (t % 2) * D:(t % 2 + 1) * D],
                                       attn_t[:, c, t * P:(t + 1) * P], w_o[:, c, :],
                                       start=(c == 0), stop=(c == NC - 1), skip_group_check=True)
                    mm.then_inc(wo_mm, 1)

            def one(b, f, last=False):
                steps = maxima(b)
                project_qk(b, 2, 0)
                project_qk(b, 2, 1)
                if f is not None:
                    turn_x1(f, 0)
                    project_qk(b, 3, 0)
                    turn_x1(f, 1)
                    project_qk(b, 3, 1)
                    mlp(f, 0, b, steps)
                    mlp(f, 1, b, steps)
                else:
                    project_qk(b, 3, 0)
                    project_qk(b, 3, 1)
                    take(steps, MX_FIRST)
                    pe.wait_ge(pool_ready, 2)
                attention(b, f, steps, last)
                out_project(b, f, last)

            pe.wait_ge(id_in, 16)
            turn_x(0, 0)
            turn_x(0, 1)
            pe.wait_ge(w_qkvo_in, 16 * 7)
            pe.wait_ge(ready, 1)
            for n in range(2):
                project_qk(0, n, 0)
                project_qk(0, n, 1)
            project_v(0, 0)
            project_v(0, 1)
            one(0, None)
            pe.wait_ge(weights_ready, 3)
            with pe.Fori(0, B - 2) as i:
                one(i + 1, i)
            one(B - 1, B - 2, last=True)
            turn_x1(B - 1, 0)
            turn_x1(B - 1, 1)
            mlp(B - 1, 0)
            mlp(B - 1, 1)

        @block.scalar
        def _(act):
            def copy_xt(b, h):
                act.wait_ge(xt_mm, b * 2 + h + 1)
                act.activation(x_t[:, :, h * BANK:(h + 1) * BANK], psum[:, 4:6, :], ACT.Copy).then_inc(xt_copied, 1)

            def copy_v(b, h):
                act.wait_ge(v_mm, b * 2 + h + 1)
                act.activation(v_ones[:, 4 * h:4 * h + 4, :, 0:HD],
                               psum[:, 0:2, :].rearrange("p b (t h d) -> p (b t) h d", t=2, d=HD),
                               ACT.Copy).then_inc(v_copied, 1)

            def turn_x1(f):
                for h in range(2):
                    act.wait_ge(x1t_mm, f * 2 + h + 1)
                    act.activation(x1_hi[:, :, h * BANK:(h + 1) * BANK], psum[:, 2 * h:2 * h + 2, :], ACT.Copy)\
                        .then_inc(x1_hi_done, 1)

            def round_part(b, n, part):
                if part == 0:
                    act.wait_ge(stored[n % 2], b * 32 + 16)
                    act.wait_ge(turned_done, b * 4 + n + 1)
                    act.activation(parts[:, n % 2, 0, :], turned, ACT.Copy).then_inc(hi_done, 1)
                else:
                    act.wait_ge(rest_done, b * 4 + n + 1)
                    act.activation(parts[:, n % 2, 1, :], rest, ACT.Copy).then_inc(mid_done, 1)

            def mlp(f, k, b=None):
                for n in range(16):
                    if b is not None and n in ROUND_AT:
                        round_part(b, *ROUND_AT[n])
                    act.wait_ge(ff_mm, f * 40 + 20 * k + n + 1)
                    h = (h1 if n < 8 else h2)[0]
                    act.activation(h[:, n % 8, :], psum[:, n % 4, :], ACT.Relu).then_inc(h_hi, 1)

            def exps(b, g, u, h):
                act.wait_ge(st_mm, b * 72 + 18 * g + 2 * u + h + 1)
                U = NU * g + u
                if U >= RING and h == 0:
                    act.wait_ge(pv_done, b * 36 + U - RING + 1)
                act.activation(probs[:, U % RING, 2 * h:2 * h + 2, :], psum[:, 2 * h:2 * h + 2, :], ACT.Exp,
                               scale=SCALE).then_inc(exp_done, 1)

            def copy_o(b, g, h):
                act.wait_ge(pv_done, b * 36 + NU * g + (5 if h == 0 else NU))
                if g > 0:
                    act.wait_ge(ot_mm, b * 4 + g)
                act.activation(o_t[:, h * BANK:(h + 1) * BANK], psum[:, 6 + h, :], ACT.Copy).then_inc(o_copied, 1)

            def attention(b, last):
                for g in range(G):
                    for u in range(NU):
                        if u == LAG and g > 0:
                            copy_o(b, g - 1, 1)
                        exps(b, g, u, 0)
                        exps(b, g, u, 1)
                        if u == XT_UNIT and g in (1, 2) and not last:
                            copy_xt(b + 1, g - 1)
                        if u == NU - 1:
                            copy_o(b, g, 0)
                copy_o(b, G - 1, 1)
                if not last:
                    copy_v(b + 1, 0)
                    copy_v(b + 1, 1)
                for h in range(2):
                    act.wait_ge(at_mm, b * 2 + h + 1)
                    act.activation(attn_t[:, :, h * BANK:(h + 1) * BANK], psum[:, 2 - 2 * h:4 - 2 * h, :], ACT.Copy)\
                        .then_inc(at_copied, 1)

            def mlp_weights():
                act.wait_ge(setup_step, 8)
                act.activation(w1[:, :, :], k1_u8, ACT.Identity, scale=w1_scale[:, 0:1], bias=w1_bias[:, 0:1])\
                    .then_inc(weights_ready, 1)
                act.activation(w2[:, :, :], k2_u8, ACT.Identity, scale=2.0, bias=minus_one[:, 0:1])\
                    .then_inc(weights_ready, 1)
                act.activation(w0[:, :, :], w0_diff, ACT.Copy, scale=s_sign[:, 0:1]).then_inc(weights_ready, 1)
                act.wait_ge(weights_ready, 3)

            def one(b, f, last=False):
                if f is not None:
                    turn_x1(f)
                    mlp(f, 0, b)
                    mlp(f, 1)
                else:
                    for n, part in ROUND_AT.values():
                        round_part(b, n, part)
                    mlp_weights()
                attention(b, last)

            for h in range(2):
                copy_xt(0, h)
            act.wait_ge(pool_ready, 1)
            for h in range(2):
                copy_v(0, h)
            one(0, None)
            with act.Fori(0, B - 2) as i:
                one(i + 1, i)
            one(B - 1, B - 2, last=True)
            turn_x1(B - 1)
            mlp(B - 1, 0)
            mlp(B - 1, 1)

        @block.gpsimd
        def _(pool):
            pool.memset(v_all[:, :, :], 1.0).then_inc(pool_ready, 1)
            pool.wait_ge(pool_ready, 1)
            pool.memset(k_st[96:128, :, :, :], 1.0).then_inc(pool_ready, 1)

            def keep_x(b):
                pool.wait_ge(x_loaded, b * 16 + 16)
                if not first(b):
                    pool.wait_ge(res_done, b * T)
                pool.sem_inc(pool_passed, 1)
                pool.tensor_copy(x_res[:, :, :], x_in[:, :, :]).then_inc(x_kept, 1)

            def times_sin(b, n):
                pool.wait_ge(swap_done, b * 4 + n + 1)
                if n or not first(b):
                    pool.wait_ge(parts_done, b * 4 + n)
                pool.tensor_tensor(rest, swapped, sin_sb[:, :], ALU.mult).then_inc(sin_done, 1)

            def less(dst, a, b):
                return pool.tensor_tensor(dst, a, b, ALU.subtract)

            def split(b, n):
                pool.wait_ge(hi_done, b * 4 + n + 1)
                less(rest, turned, parts[:, n % 2, 0, :]).then_inc(rest_done, 1)
                pool.wait_ge(mid_done, b * 4 + n + 1)
                less(parts[:, n % 2, 2, :], rest, parts[:, n % 2, 1, :]).then_inc(parts_done, 1)

            def inv_std(done, eps_ready, n, dst, src, width):
                pool.wait_ge(eps_ready, n)
                pool.tensor_tensor(dst, src, minus_half[:, 0:width], ALU.pow).then_inc(done, 1)

            def masks(b, g, which=MASKED):
                for u in which:
                    pool.wait_ge(exp_done, b * 72 + 18 * g + 2 * u + 2)
                    pool.sem_inc(pool_passed, 1)
                    for col in DIAG[u]:
                        blk = probs[:, (NU * g + u) % RING, :, col:col + P]
                        op = pool.affine_select(out=blk, in_=blk, compare_op=ALU.is_ge, fill=0.0, base=0,
                                                pattern=[[0, HG], [1, P]], channel_multiplier=-1)
                    op.then_inc(mask_done, 1)

            def one(b, f, last=False):
                keep_x(b)
                times_sin(b, 2)
                split(b, 2)
                times_sin(b, 3)
                split(b, 3)
                if f is not None:
                    inv_std(rstd2_done, eps2_done, f * 2 + 1, rstd2[:, :], var_eps2[:, :], 4)
                masks(b, 0, MASKED[:3])
                if f is not None:
                    inv_std(rstd2_done, eps2_done, f * 2 + 2, rstd2[:, :], var_eps2[:, :], 4)
                masks(b, 0, MASKED[3:])
                for g in range(1, G - 1):
                    masks(b, g)
                masks(b, G - 1, MASKED[:1])
                if not last:
                    times_sin(b + 1, 0)
                masks(b, G - 1, MASKED[1:])
                if not last:
                    times_sin(b + 1, 1)
                for h in range(2):
                    inv_std(rstd_done, eps_done, b * 2 + h + 1, rstd[:, 4 * h:4 * h + 4], var_eps[:, 4 * h:4 * h + 4], 4)

            pool.wait_ge(pool_ready, 2)
            pool.wait_ge(ready, 1)
            pool.wait_ge(tables_in, 16 * 3)
            times_sin(0, 0)
            times_sin(0, 1)
            one(0, None)
            with pool.Fori(0, B - 2) as i:
                one(i + 1, i)
            one(B - 1, B - 2, last=True)
            inv_std(rstd2_done, eps2_done, (B - 1) * 2 + 1, rstd2[:, :], var_eps2[:, :], 4)
            inv_std(rstd2_done, eps2_done, (B - 1) * 2 + 2, rstd2[:, :], var_eps2[:, :], 4)

        @block.vector
        def _(dve):
            dumps = [0]
            SWAP = [i ^ 1 for i in range(32)]

            def rope(b, n):
                bank = 6 if n == 3 else 4
                ps = psum[:, bank:bank + 2, :].rearrange("p b n -> p (b n)")
                dve.wait_ge(qk_mm, b * 4 + n + 1)
                dve.sem_inc(dve_passed, 1)
                dve.stream_shuffle(swapped, ps, SWAP).then_inc(swap_done, 1)
                yield
                if n or not first(b):
                    dve.wait_ge(parts_done if n == 0 else rest_done, b * 4 + n)
                dve.tensor_tensor(turned, ps, cos_sb[:, :], ALU.mult).then_inc(cos_done, 1)
                yield
                dve.wait_ge(cos_done, b * 4 + n + 1)
                dve.wait_ge(sin_done, b * 4 + n + 1)
                dve.tensor_tensor(turned, turned, rest, ALU.add).then_inc(turned_done, 1)
                yield
                if n >= 2:
                    return
                if not first(b):
                    dve.wait_ge(stored[n % 2], b * 32)
                dve.wait_ge(turned_done, b * 4 + n + 1)
                dve.tensor_copy(parts[:, n % 2, 0, :], turned).then_inc(hi_done, 1)
                yield
                dve.wait_ge(hi_done, b * 4 + n + 1)
                dve.tensor_tensor(rest, turned, parts[:, n % 2, 0, :], ALU.subtract).then_inc(rest_done, 1)
                yield
                dve.wait_ge(rest_done, b * 4 + n + 1)
                dve.tensor_copy(parts[:, n % 2, 1, :], rest).then_inc(mid_done, 1)
                yield
                dve.wait_ge(mid_done, b * 4 + n + 1)
                dve.tensor_tensor(parts[:, n % 2, 2, :], rest, parts[:, n % 2, 1, :], ALU.subtract)\
                    .then_inc(parts_done, 1)
                yield

            def turn_x1(f):
                for h in range(2):
                    dve.wait_ge(x1_hi_done, f * 2 + h + 1)
                    dve.tensor_tensor(x1_lo[:, :, h * BANK:(h + 1) * BANK], psum[:, 2 * h:2 * h + 2, :],
                                      x1_hi[:, :, h * BANK:(h + 1) * BANK], ALU.subtract).then_inc(x1_lo_done, 1)

            def mlp(f, k, late=None, steps=None, norm_of_before=None, norm_of_this=None):
                def lo(n):
                    h = h1 if n < 8 else h2
                    dve.wait_ge(h_hi, f * 32 + 16 * k + n + 1)
                    dve.scalar_tensor_tensor(out=h[1][:, n % 8, :], in0=psum[:, n % 4, :], scalar=0.0,
                                             in1=h[0][:, n % 8, :], op0=ALU.max, op1=ALU.subtract)\
                        .then_inc(h_lo, 1)

                for n in range(8):
                    lo(n)
                for n in range(8):
                    if n:
                        lo(7 + n)
                    others, count = (late, ROPE_BESIDE[n]) if k == 0 else (norm_of_before, NORM_BESIDE[n])
                    for i in range(max(MX_BESIDE[k][n], 1)):
                        take(others, spread(count, i, max(MX_BESIDE[k][n], 1)))
                        take(steps, min(MX_BESIDE[k][n], 1))
                lo(15)
                if k == 0:
                    dve.wait_ge(out_stored, f * 32 + 16)
                else:
                    dve.wait_ge(out_stored, f * 32 + 32)
                for t in range(4):
                    take(steps, MX_BESIDE[k][8 + t])
                    dve.wait_ge(ff_mm, f * 40 + 20 * k + 17 + t)
                    dve.scalar_tensor_tensor(out=y[:, t, :], in0=psum[:, 6 + t % 2, 0:D], scalar=factor[:, 0:1],
                                             in1=x1[:, 4 * k + t, :], op0=ALU.mult, op1=ALU.add)\
                        .then_inc(y_done, 1)
                    take(norm_of_this, 1)

            def norm2(f, k):
                for t in range(4):
                    dve.wait_ge(y_done, f * 8 + 4 * k + t + 1)
                    dve.bn_stats(stats2[:, t, :], y[:, t, :]).then_inc(stat2_done, 1)
                    yield
                for t in range(4):
                    dve.wait_ge(stat2_done, f * 8 + 4 * k + t + 1)
                    dve.sem_inc(dve_passed, 1)
                    dve.bn_aggr(mean_var2[:, t, :], stats2[:, t, :]).then_inc(aggr2_done, 1)
                dve.wait_ge(aggr2_done, f * 8 + 4 * k + 4)
                dve.tensor_scalar(var_eps2[:, :], mean_var2[:, :, 1], EPS, None, ALU.add).then_inc(eps2_done, 1)
                yield
                for t in range(4):
                    if t == 0:
                        dve.wait_ge(rstd2_done, f * 2 + k + 1)
                    dve.tensor_scalar(y[:, t, :], y[:, t, :], mean_var2[:, t, 0:1], rstd2[:, t:t + 1],
                                      ALU.subtract, ALU.mult).then_inc(out_done, 1)
                    yield

            def maxima(b):
                for e, (g, j, u) in enumerate(MX_ORDER):
                    if j is None:
                        split_maxima(b, g, e)
                        yield
                        continue
                    if j == u == 0 and (g >= 2 or not first(b)):
                        dve.wait_ge(m_found, b * 4 + g - 1)
                    dve.wait_ge(mx_mm, b * MXB + e + 1)
                    bank = mx_bank(b, e)
                    for t, a, end, col in MX_UNITS[u]:
                        diag = end == (t + 1) * P
                        wide = end - a - (P if diag else 0)
                        if first(b):
                            place = a // BANK if wide else 2
                            op = dve.tensor_reduce(mx[:, g % 2, j, t, place:place + 1],
                                                   psum[:, bank, col:col + end - a], AX.X, ALU.max)
                            continue
                        if wide:
                            op = dve.tensor_reduce(mx[:, g % 2, j, t, a // BANK:a // BANK + 1],
                                                   psum[:, bank, col:col + wide], AX.X, ALU.max)
                        if diag:
                            dumps[0] += 1
                            op = dve.tensor_tensor_reduce(dump[:, dumps[0] % 4, :],
                                                          psum[:, bank, col + wide:col + wide + P],
                                                          tri_sb[:, :], 1.0, LOWEST, ALU.add, ALU.max,
                                                          mx[:, g % 2, j, t, 2:3])
                    op.then_inc(mx_read, 1)
                    if (j, u) == (HG - 1, NMX - 1):
                        dve.wait_ge(mx_read, b * MXB + e + 1)
                        if g:
                            dve.wait_ge(mx_mm, b * MXB + TURN_AT[g - 1] + 1)
                        elif not first(b):
                            dve.wait_ge(mx_mm, b * MXB)
                        dve.tensor_reduce(m_col[:, 0:HG * T], mx[:, g % 2].rearrange("p j t a -> p (j t) a"), AX.X,
                                          ALU.max).then_inc(m_found, 1)
                    yield

            def split_maxima(b, g, e):
                mt = psum[0:HG * T, mx_bank(b, e), 0:P]
                dve.wait_ge(mx_mm, b * MXB + e + 1)
                dve.wait_ge(m_rows, b * 192 + 48 * g)
                dve.tensor_scalar(m_parts[:, 0, :], mt, -1.0, None, ALU.mult).then_inc(m_hi, 1)
                dve.wait_ge(m_hi, b * 4 + g + 1)
                dve.scalar_tensor_tensor(out=m_rest[:, :], in0=mt, scalar=-1.0, in1=m_parts[:, 0, :],
                                         op0=ALU.mult, op1=ALU.subtract).then_inc(mx_read, 1)
                dve.wait_ge(mx_read, b * MXB + e + 1)
                dve.tensor_copy(m_parts[:, 1, :], m_rest[:, :]).then_inc(m_mid, 1)
                dve.wait_ge(m_mid, b * 4 + g + 1)
                dve.tensor_tensor(m_parts[:, 2, :], m_rest[:, :], m_parts[:, 1, :], ALU.subtract)\
                    .then_inc(m_split, 1)

            def normalise(b, g):
                q = 4 if g < G - 1 else 2
                o = psum[:, q:q + 2, :].rearrange("p b (t j d) -> p (b t) j d", t=4, j=HG)
                dve.wait_ge(ot_mm, b * 4 + g + 1)
                if g or not first(b):
                    dve.wait_ge(normed, b * 4 + g)
                dve.reciprocal(recip[:, :, :], o[:, :, :, HD]).then_inc(recip_done, 1)
                dve.wait_ge(recip_done, b * 4 + g + 1)
                if g == 0 and not first(b):
                    dve.wait_ge(at_mm, b * 2)
                dst = attn[:, :, HG * HD * g:HG * HD * (g + 1)].rearrange("p t (j d) -> p t j d", j=HG)
                dve.tensor_tensor(dst, o[:, :, :, 0:HD],
                                  recip[:, :, :].unsqueeze(3).to_broadcast([P, T, HG, HD]), ALU.mult)\
                    .then_inc(normed, 1)

            def attention(b, f, steps, last):
                second_norm = norm2(f, 1) if f is not None else None
                for g in range(G - 1):
                    for u in range(NU):
                        take(steps, (MX_AT if f is not None else MX_AT_FIRST)[NU * g + u])
                        if g == 0 and u < len(NORM_AT):
                            take(second_norm, NORM_AT[u])
                        if u == OT_UNIT and g > 0:
                            normalise(b, g - 1)
                        if g == G - 2 and u == XT_UNIT + 1:
                            take(steps, 1)
                ahead = None if last else rope(b + 1, 0)
                take(ahead, 5)
                normalise(b, G - 2)
                if not last:
                    run(ahead)
                    run(rope(b + 1, 1))
                normalise(b, G - 1)

            def norm1(b):
                for h in range(2):
                    tiles = range(4 * h, 4 * h + 4)
                    for t in tiles:
                        dve.wait_ge(wo_mm, b * T + t // 2 * 2 + 2)
                        if t == 0:
                            dve.wait_ge(x_kept, b + 1)
                            if not first(b):
                                dve.wait_ge(y_done, b * 8)
                                dve.wait_ge(x1t_mm, b * 2)
                        dve.tensor_tensor(x1[:, t, :], psum[:, 4 + t // 2, (t % 2) * D:(t % 2 + 1) * D],
                                          x_res[:, t, :], ALU.add).then_inc(res_done, 1)
                    for t in tiles:
                        dve.wait_ge(res_done, b * T + t + 1)
                        dve.bn_stats(stats[:, t, :], x1[:, t, :]).then_inc(stat_done, 1)
                    if h == 1:
                        scale1(b, 0)
                    for t in tiles:
                        dve.wait_ge(stat_done, b * T + t + 1)
                        dve.sem_inc(dve_passed, 1)
                        dve.bn_aggr(mean_var[:, t, :], stats[:, t, :]).then_inc(aggr_done, 1)
                    dve.wait_ge(aggr_done, b * T + 4 * h + 4)
                    dve.tensor_scalar(var_eps[:, 4 * h:4 * h + 4], mean_var[:, 4 * h:4 * h + 4, 1], EPS, None,
                                      ALU.add).then_inc(eps_done, 1)
                scale1(b, 1)

            def scale1(b, h):
                dve.wait_ge(rstd_done, b * 2 + h + 1)
                for t in range(4 * h, 4 * h + 4):
                    dve.tensor_scalar(x1[:, t, :], x1[:, t, :], mean_var[:, t, 0:1], rstd[:, t:t + 1],
                                      ALU.subtract, ALU.mult).then_inc(x1_done, 1)

            def run(gen):
                for _ in gen:
                    pass

            def chain(*gens):
                for gen in gens:
                    yield from gen

            def one(b, f, last=False):
                late, steps = chain(rope(b, 2), rope(b, 3)), maxima(b)
                if f is not None:
                    turn_x1(f)
                    mlp(f, 0, late, steps)
                    mlp(f, 1, None, steps, norm2(f, 0))
                else:
                    for n in MX_ROPE_FIRST:
                        take(late, 1)
                        take(steps, n)
                    take(steps, MX_FIRST - sum(MX_ROPE_FIRST))
                attention(b, f, steps, last)
                norm1(b)

            dve.memset(m_col[:, :], 0.0)
            dve.memset(minus_half[:, :], -0.5)
            dve.memset(minus_one[:, :], -1.0)
            dve.memset(mx[:, :, :, :, :], LOWEST).then_inc(ready, 1)
            dve.wait_ge(tables_in, 16 * 3)
            dve.wait_ge(id_in, 16)
            dve.tensor_copy(id_bf[:, :], id_sb[:, :]).then_inc(mask_ready, 1)
            dve.tensor_copy(tri_bf[:, :], tri_sb[:, :]).then_inc(mask_ready, 1)
            run(rope(0, 0))
            run(rope(0, 1))
            dve.wait_ge(w_in, 16 * 6)
            dve.tensor_tensor(w0_diff, k0_u8[:, 0:2, :], k0_u8[:, 2:4, :], ALU.subtract)\
                .then_inc(setup_step, 1)
            dve.tensor_scalar(s_sign[:, :], s_in[:, :], 0.0, 2.0, ALU.is_ge, ALU.mult).then_inc(setup_step, 1)
            dve.wait_ge(setup_step, 2)
            dve.tensor_scalar(s_sign[:, :], s_sign[:, :], -1.0, None, ALU.add).then_inc(setup_step, 1)
            dve.wait_ge(setup_step, 3)
            dve.tensor_scalar(w1_scale[:, :], s_sign[:, 1:2], 2.0 * W1_SCALE, None, ALU.mult).then_inc(setup_step, 1)
            dve.tensor_scalar(w1_bias[:, :], s_sign[:, 1:2], -W1_SCALE, None, ALU.mult).then_inc(setup_step, 1)
            dve.tensor_tensor(s_abs[:, :], s_in[:, :], s_sign[:, :], ALU.mult).then_inc(setup_step, 1)
            dve.wait_ge(setup_step, 6)
            dve.tensor_tensor(s_prod[:, :], s_abs[:, 0:1], s_abs[:, 1:2], ALU.mult).then_inc(setup_step, 1)
            dve.wait_ge(setup_step, 7)
            dve.scalar_tensor_tensor(out=factor[:, :], in0=s_prod[:, :], scalar=OUT_FACTOR, in1=s_in[:, 2:3],
                                     op0=ALU.mult, op1=ALU.mult).then_inc(setup_step, 1)
            one(0, None)
            with dve.Fori(0, B - 2) as i:
                one(i + 1, i)
            one(B - 1, B - 2, last=True)
            turn_x1(B - 1)
            mlp(B - 1, 0)
            last_norm = norm2(B - 1, 1)
            mlp(B - 1, 1, norm_of_before=norm2(B - 1, 0), norm_of_this=last_norm)
            run(last_norm)


NAMES = ("x", "wq", "wk", "wv", "wo", "k0", "k1", "k2", "s0", "s1", "s2")


def rope_tables():
    inv = (np.float32(1.0) / np.float32(10000.0) ** (np.arange(0, HD, 2, dtype=np.float32) / np.float32(HD)))
    ang = (np.arange(S, dtype=np.float32)[None, :] * inv.astype(np.float32)[:, None]).astype(np.float32)
    row = np.arange(P) % HD
    a = ang[row // 2]
    sign = np.where(row % 2 == 0, -1.0, 1.0)[:, None]
    return np.cos(a.astype(np.float64)).astype(np.float32), (np.sin(a.astype(np.float64)) * sign).astype(np.float32)


def kernel(L0_attn_x, L0_attn_wq, L0_attn_wk, L0_attn_wv, L0_attn_wo, L0_ffn_k0, L0_ffn_k1, L0_ffn_k2,
           L0_ffn_s0, L0_ffn_s1, L0_ffn_s2):
    import concourse.bacc as bacc
    from concourse.bass_utils import run_bass_kernel_spmd

    cos, sin = rope_tables()
    row, col = np.arange(P)[:, None], np.arange(P)[None, :]
    arrays = {
        "x": np.ascontiguousarray(L0_attn_x),
        "wq": np.ascontiguousarray(L0_attn_wq),
        "wk": np.ascontiguousarray(L0_attn_wk),
        "wv": np.ascontiguousarray(L0_attn_wv),
        "wo": np.ascontiguousarray(L0_attn_wo),
        "k0": np.ascontiguousarray(L0_ffn_k0),
        "k1": np.ascontiguousarray(L0_ffn_k1),
        "k2": np.ascontiguousarray(L0_ffn_k2),
        "s0": np.asarray(L0_ffn_s0).reshape(1),
        "s1": np.asarray(L0_ffn_s1).reshape(1),
        "s2": np.asarray(L0_ffn_s2).reshape(1),
        "cos": cos,
        "sin": sin,
        "ident": np.eye(P, dtype=np.float32),
        "tri": np.where(col <= row, 0.0, -1.0e38).astype(np.float32),
    }
    nc = bacc.Bacc("TRN2", target_bir_lowering=False, num_devices=1)
    ins = [nc.dram_tensor(f"in_{n}", a.shape, mybir.dt.from_np(a.dtype), kind="ExternalInput").ap()
           for n, a in arrays.items()]
    out = nc.dram_tensor("out", (B, S, D), F32, kind="ExternalOutput").ap()
    scratch = nc.dram_tensor("scratch", (2, 2, 3, P, S), BF16).ap()
    build(nc, *ins, out, scratch)
    r = run_bass_kernel_spmd(nc, [{f"in_{n}": a for n, a in arrays.items()}], core_ids=[0])
    return r.results[0]["out"]
```
